# Optimizing a Trainium2 kernel written in Bass

```python
import numpy as np
import jax
import jax.numpy as jnp

def _softmax(x, axis=-1):
    return jax.nn.softmax(x, axis=axis)
def _gelu(x):
    return jax.nn.gelu(x, approximate=True)
def _silu(x):
    return jax.nn.silu(x)
def _sigmoid(x):
    return jax.nn.sigmoid(x)
def _layernorm(x, axis=-1, eps=1e-5):
    m = jnp.mean(x, axis=axis, keepdims=True)
    v = jnp.var(x, axis=axis, keepdims=True)
    return (x - m) / jnp.sqrt(v + eps)
def _scatter_add(tgt, idx, src, axis=0):
    return tgt.at[idx].add(src)
def _segment_sum(src, seg, n):
    return jax.ops.segment_sum(src, seg, n)

kernel_name = 'mk_conv_seq_d2_conv_nchw512_610ad9'

def setup_inputs(seed: int = 0):
    np.random.seed(seed)
    _w = jnp.asarray
    def _rec_inputs():
        import jax
        import jax.numpy as jnp
        _gk = jax.random.key(seed)
        x = -0.0002928 + 1 * jax.random.normal(jax.random.fold_in(_gk, 1), (8, 512, 32, 32), jnp.float32)
        return x
    x = _rec_inputs()
    def _L0_conv_setup():
        import jax, jax.numpy as jnp
        import numpy as np
        import math
        B, C, H, W = (8, 512, 32, 32)
        NUM_HEADS = 8
        GROUP = 32
        EPS = 1e-05

        def group_norm(x, w, b):
            Bx, Cx, Hx, Wx = x.shape
            xg = x.reshape(Bx, GROUP, Cx // GROUP, Hx, Wx)
            mean = xg.mean(axis=(2, 3, 4), keepdims=True)
            var = xg.var(axis=(2, 3, 4), keepdims=True)
            xg = (xg - mean) * jax.lax.rsqrt(var + EPS)
            x = xg.reshape(Bx, Cx, Hx, Wx)
            return x * w[None, :, None, None] + b[None, :, None, None]
        key = jax.random.key(seed)
        k1, k2, k3 = jax.random.split(key, 3)
        x = jax.random.normal(k1, (B, C, H, W), dtype=jnp.float32)
        norm_w = jnp.ones((C,), dtype=jnp.float32)
        norm_b = jnp.zeros((C,), dtype=jnp.float32)
        qkv_w = jax.random.normal(k2, (3 * C, C), dtype=jnp.float32) * (1.0 / math.sqrt(C))
        proj_w = jax.random.normal(k3, (C, C), dtype=jnp.float32) * (1.0 / math.sqrt(C))
        proj_b = jnp.zeros((C,), dtype=jnp.float32)
        return {'x': x, 'norm_w': norm_w, 'norm_b': norm_b, 'qkv_w': qkv_w, 'proj_w': proj_w, 'proj_b': proj_b}
    _L0_conv_all = _L0_conv_setup()
    _L0_conv_in = {k: v for k, v in _L0_conv_all.items() if k in ('norm_w', 'norm_b', 'qkv_w', 'proj_w', 'proj_b', )}
    del _L0_conv_all

    def _L1_conv_setup():
        import jax, jax.numpy as jnp
        import numpy as np
        B, C, H, W = (4, 512, 64, 64)
        RED = 8
        D = C // RED
        key = jax.random.key(seed)
        k0, k1, k2, k3, k4, k5 = jax.random.split(key, 6)
        x = jax.random.normal(k0, (B, C, H, W), dtype=jnp.float32)
        Wq = jax.random.normal(k1, (D, C), dtype=jnp.float32) * 0.02
        bq = jax.random.normal(k2, (D,), dtype=jnp.float32) * 0.02
        Wv = jax.random.normal(k3, (C, C), dtype=jnp.float32) * 0.02
        bv = jax.random.normal(k4, (C,), dtype=jnp.float32) * 0.02
        gamma = jax.random.normal(k5, (1,), dtype=jnp.float32) * 0.1
        return {'x': x, 'Wq': Wq, 'bq': bq, 'Wv': Wv, 'bv': bv, 'gamma': gamma}
    _L1_conv_all = _L1_conv_setup()
    _L1_conv_in = {k: v for k, v in _L1_conv_all.items() if k in ('Wq', 'bq', 'Wv', 'bv', 'gamma', )}
    del _L1_conv_all

    return {
        "x": x,
        "L0_conv_norm_w": _L0_conv_in["norm_w"],
        "L0_conv_norm_b": _L0_conv_in["norm_b"],
        "L0_conv_qkv_w": _L0_conv_in["qkv_w"],
        "L0_conv_proj_w": _L0_conv_in["proj_w"],
        "L0_conv_proj_b": _L0_conv_in["proj_b"],
        "L1_conv_Wq": _L1_conv_in["Wq"],
        "L1_conv_bq": _L1_conv_in["bq"],
        "L1_conv_Wv": _L1_conv_in["Wv"],
        "L1_conv_bv": _L1_conv_in["bv"],
        "L1_conv_gamma": _L1_conv_in["gamma"],
    }

def reference(x, L0_conv_norm_w, L0_conv_norm_b, L0_conv_qkv_w, L0_conv_proj_w, L0_conv_proj_b, L1_conv_Wq, L1_conv_bq, L1_conv_Wv, L1_conv_bv, L1_conv_gamma):
    import jax
    import jax.numpy as jnp
    def _L0_conv_ref(x, norm_w, norm_b, qkv_w, proj_w, proj_b):
        import jax, jax.numpy as jnp
        import numpy as np
        import math
        B, C, H, W = (8, 512, 32, 32)
        NUM_HEADS = 8
        GROUP = 32
        EPS = 1e-05

        def group_norm(x, w, b):
            Bx, Cx, Hx, Wx = x.shape
            xg = x.reshape(Bx, GROUP, Cx // GROUP, Hx, Wx)
            mean = xg.mean(axis=(2, 3, 4), keepdims=True)
            var = xg.var(axis=(2, 3, 4), keepdims=True)
            xg = (xg - mean) * jax.lax.rsqrt(var + EPS)
            x = xg.reshape(Bx, Cx, Hx, Wx)
            return x * w[None, :, None, None] + b[None, :, None, None]
        Bx, Cx, Hx, Wx = x.shape
        N = Hx * Wx
        head_dim = Cx // NUM_HEADS
        xn = group_norm(x, norm_w, norm_b)
        qkv = jnp.einsum('bchw,oc->bohw', xn, qkv_w)
        qkv = qkv.reshape(Bx * NUM_HEADS, 3 * head_dim, N)
        q, k, v = jnp.split(qkv, 3, axis=1)
        scale = 1.0 / math.sqrt(math.sqrt(head_dim))
        attn = jnp.einsum('bct,bcs->bts', q * scale, k * scale)
        attn = jax.nn.softmax(attn, axis=-1)
        h = jnp.einsum('bts,bcs->bct', attn, v)
        h = h.reshape(Bx, Cx, Hx, Wx)
        h = jnp.einsum('bchw,oc->bohw', h, proj_w) + proj_b[None, :, None, None]
        return h + x

    def _L1_conv_ref(x, Wq, bq, Wv, bv, gamma):
        import jax, jax.numpy as jnp
        import numpy as np
        B, C, H, W = (4, 512, 64, 64)
        RED = 8
        D = C // RED
        b, c, h, w = x.shape
        n = h * w
        xf = x.reshape(b, c, n)
        q = jnp.einsum('dc,bcn->bnd', Wq, xf) + bq
        k = jnp.einsum('dc,bcn->bdn', Wq, xf) + bq[:, None]
        energy = jnp.einsum('bnd,bdm->bnm', q, k)
        attention = jax.nn.softmax(energy, axis=-1)
        v = jnp.einsum('ec,bcn->ben', Wv, xf) + bv[:, None]
        out = jnp.einsum('bcj,bij->bci', v, attention)
        out = gamma[0] * out.reshape(b, c, h, w) + x
        return out

    def _gn(v, G=32, eps=1e-5):
        B_, C_, H_, W_ = v.shape
        g = v.reshape(B_, G, C_ // G, H_, W_)
        m = jnp.mean(g, axis=(2, 3, 4), keepdims=True)
        s = jnp.var(g, axis=(2, 3, 4), keepdims=True)
        return ((g - m) / jnp.sqrt(s + eps)).reshape(v.shape)

    def _ln_c(v, eps=1e-6):
        m = jnp.mean(v, axis=1, keepdims=True)
        s = jnp.var(v, axis=1, keepdims=True)
        return (v - m) / jnp.sqrt(s + eps)

    def _ln_t(v, eps=1e-5):
        m = jnp.mean(v, axis=-1, keepdims=True)
        s = jnp.var(v, axis=-1, keepdims=True)
        return (v - m) / jnp.sqrt(s + eps)

    def _to_tokens(v):
        B_, C_, H_, W_ = v.shape
        return v.reshape(B_, C_, H_ * W_).transpose(0, 2, 1)
    def _from_tokens(t, like):
        B_, C_, H_, W_ = like.shape
        return t.transpose(0, 2, 1).reshape(B_, C_, H_, W_)

    x = _L0_conv_ref(x, L0_conv_norm_w, L0_conv_norm_b, L0_conv_qkv_w, L0_conv_proj_w, L0_conv_proj_b)
    x = _L1_conv_ref(x, L1_conv_Wq, L1_conv_bq, L1_conv_Wv, L1_conv_bv, L1_conv_gamma)
    return x


_drawn_inputs = setup_inputs


def setup_inputs(seed=0):
    import zlib

    import numpy as np

    out = dict(_drawn_inputs(seed))
    spreads = {'L0_conv_norm_w': (1.0, 0.2), 'L0_conv_norm_b': (0.0, 0.1), 'L0_conv_proj_b': (0.0, 0.1)}
    factors = {'L1_conv_Wq': 8.0, 'L1_conv_bq': 8.0, 'L1_conv_bv': 45.906}
    for name, (base, spread) in spreads.items():
        noise = np.random.default_rng([zlib.crc32(name.encode()), seed]).standard_normal(out[name].shape)
        drawn = base * np.exp(spread * noise) if base else spread * noise
        out[name] = jnp.asarray(drawn.astype(out[name].dtype))
    for name, factor in factors.items():
        out[name] = (out[name] * factor).astype(out[name].dtype)
    return out
```

```python
from contextlib import ExitStack

import numpy as np

import concourse.bass as bass
from concourse import mybir

B, C, N = 8, 512, 1024
P = 128
KT = C // P
ST = N // P
HEADS = 8
D = C // HEADS
HALF = 512
NH = N // HALF
GROUPS = 32
EPS = 1e-5
SCALE = float(D) ** -0.5

F32 = mybir.dt.float32
F32R = mybir.dt.float32r
ALU = mybir.AluOpType
ACT = mybir.ActivationFunctionType
AX_X = mybir.AxisListType.X

MAX_BETWEEN = {3: 3}
MAX_AFTER = {0: 0, 1: 1, 2: 2, 3: 4, 4: 5, 5: 6, 6: 7}
PROJ_BETWEEN = {1: 0, 2: 1, 4: 2, 5: 3}
PROJ_HEADS = (3, 5, 7)
SCALE_AT = {1: 4, 0: 6}


def psum_uses():
    s0, s1, acc, misc = [], [], [], []
    acc += [("mean",), ("var",)]
    for j in range(ST):
        (s0, s1)[j % 2].append(("v", j))
    misc += [("qk", 0), ("qk", 1)]
    for t in range(ST):
        (misc, acc)[t % 2].append(("max", 0, t))
    s0.append(("row", 0))
    for h in range(HEADS):
        acc.append(("pv", h))
        for j in range(ST):
            (s0, s1)[j % 2].append(("s", h, j))
            if h + 1 < HEADS and j in MAX_BETWEEN:
                misc.append(("max", h + 1, MAX_BETWEEN[j]))
            if h in PROJ_HEADS and j in PROJ_BETWEEN:
                misc.append(("proj", h // 2 - 1, PROJ_BETWEEN[j]))
            if h + 1 < HEADS and j in MAX_AFTER:
                misc.append(("max", h + 1, MAX_AFTER[j]))
        if h + 1 < HEADS:
            s0.append(("row", h + 1))
        if h + 2 < HEADS:
            misc.append(("qk", h + 2))
    for m in range(KT):
        (misc, s0)[m % 2].append(("proj", KT - 1, m))
    acc.append(("g",))
    for j in range(ST):
        (s0, s1)[j % 2].append(("v1", j))
    for t in range(ST):
        (misc, acc)[t % 2].append(("max", HEADS, t))
    s0.append(("row", HEADS))
    for n in range(NH):
        s1.append(("den", n))
        acc.append(("o", n))
        misc.append(("o", n))
    return {"s0": s0, "s1": s1, "acc": acc, "misc": misc}


USES = psum_uses()
TILES = HEADS * ST + NH * ST
DVE_LINKS = 4 + 6 * NH


def pair_of(what):
    return next(pair for pair in USES if what in USES[pair])


def filling(b, what, pair=None):
    pair = pair or pair_of(what)
    signalled = [w for w in USES[pair] if not on_pv_done(w, pair)]
    return b * len(signalled) + signalled.index(what) + 1


def on_pv_done(what, pair):
    return what[0] == "pv" or (what[0] == "o" and pair == "misc")


def use(b, what, pair=None, done=0):
    pair = pair or pair_of(what)
    return 1 + b * len(USES[pair]) + USES[pair].index(what) + done


def attention_kernel(nc, x, wqk, wv, wv1, wp, wq1, pb, norm_w, norm_b, bv1, bq1, gamma, group, ident, out):
    with ExitStack() as ctx:
        def sb(name, shape, dt=F32):
            return ctx.enter_context(nc.sbuf_tensor(name, shape, dt))

        def sem(name):
            return ctx.enter_context(nc.semaphore(name))

        qk_hl = nc.dram_tensor("qk_hl", [HEADS + 1, P, 2, KT * P], F32, kind="Internal").ap()
        v_hl = nc.dram_tensor("v_hl", [P, 2, KT * C], F32, kind="Internal").ap()
        v1_hl = nc.dram_tensor("v1_hl", [P, 2, KT * C], F32, kind="Internal").ap()
        p_hl = nc.dram_tensor("p_hl", [KT, P, 2, C], F32, kind="Internal").ap()

        rden_row = nc.dram_tensor("rden_row", [2, N], F32, kind="Internal").ap()

        x_in = sb("x_in", [P, KT, N])
        x_mid = sb("x_mid", [P, KT, N])
        xh = sb("xh", [P, KT, N], F32R)
        xl = sb("xl", [P, KT, N], F32R)
        w_qk = [sb(f"w_qk{i}", [P, 2, KT, P], F32R) for i in range(2)]
        w_v = sb("w_v", [P, 2, KT, C], F32R)
        w_p = sb("w_p", [P, 2, C], F32R)
        k_hl = [sb(f"k_hl{i}", [P, N], F32R) for i in range(2)]
        q_hh = [sb(f"q_hh{i}", [P, N], F32R) for i in range(2)]
        k_h1 = [sb(f"k_h1{i}", [P, N], F32R) for i in range(2)]
        q_lm = [sb(f"q_lm{i}", [P, N], F32R) for i in range(2)]
        vh = sb("vh", [P, ST, HEADS // 2, 3, D], F32R)
        vl = sb("vl", [P, ST, HEADS // 2, 3, D], F32R)
        ef = sb("ef", [P, N])
        eh = [sb(f"eh{i}", [P, N], F32R) for i in range(2)]
        el = [sb(f"el{i}", [P, N], F32R) for i in range(2)]
        hf = sb("hf", [P, N])
        hh = sb("hh", [P, N], F32R)
        hl = sb("hl", [P, N], F32R)
        den_c, rden_c = sb("den_c", [P, N // P]), sb("rden_c", [P, N // P])
        ones = sb("ones", [P, P], F32R)
        eye = sb("eye", [P, P])
        grp = sb("grp", [P, P])
        mx = [sb(f"mx{i}", [P, ST]) for i in range(2)]
        cols = sb("cols", [P, 5, KT])
        pb_c, nw_c, nb_c, bv_c, gb_c = (cols[:, i, :] for i in range(5))
        scal = sb("scal", [P, 2])
        bq_c, gamma_c = scal[:, 0:1], scal[:, 1:2]
        stats = sb("stats", [P, KT, NH, 6])
        mv = sb("mv", [P, KT, 2])
        gm = sb("gm", [P, 7, KT])
        mean_c, dev_c, var_c, rstd_c, fac_c, minus_half, unused = (gm[:, i, :] for i in range(7))

        bank = {n: ctx.enter_context(nc.psum_tensor(f"ps_{n}", [P, N], F32)) for n in USES}
        S = ("s0", "s1")

        filled = {n: sem(f"{n}_filled") for n in bank}
        drained = {n: sem(f"{n}_drained") for n in bank}
        w_in, w_hi, w_split, w_out = sem("w_in"), sem("w_hi"), sem("w_split"), sem("w_out")
        consts_in, ones_set, x_loaded = sem("consts_in"), sem("ones_set"), sem("x_loaded")
        stat_ready, rstd_ready, y_ready = sem("stat_ready"), sem("rstd_ready"), sem("y_ready")
        norm_hi, norm_lo = sem("norm_hi"), sem("norm_lo")
        v_hi, mid_hi, mid_lo = sem("v_hi"), sem("mid_hi"), sem("mid_lo")
        wqk_loaded = [sem(f"wqk_loaded{i}") for i in range(2)]
        wv_loaded, wp_loaded = sem("wv_loaded"), sem("wp_loaded")
        qk_hi, qk_twin = sem("qk_hi"), [sem(f"qk_twin{i}") for i in range(2)]
        e_hi, e_lo, hi_done, pv_done = sem("e_hi"), sem("e_lo"), sem("hi_done"), sem("pv_done")
        h_hi, h_lo, h_scaled = sem("h_hi"), sem("h_lo"), sem("h_scaled")
        den_spread, rden_ready, rden_out, rden_back = (
            sem(n) for n in ("den_spread", "rden_ready", "rden_out", "rden_back")
        )
        t1_filled, t1_drained = sem("t1_filled"), sem("t1_drained")
        out_ready, out_done, dve_step = sem("out_ready"), sem("out_done"), sem("dve_step")

        def head_v(tile, h, j):
            start = (h // 2) * 3 * D + (h % 2) * D
            return tile[:, j].rearrange("p a c d -> p (a c d)")[:, start : start + P]

        def rows_of(h):
            return slice(D * (h % 2), D * (h % 2) + D)

        def half(n):
            return slice(n * HALF, (n + 1) * HALF)

        def by_partition(w):
            return w.rearrange("p k n -> p (k n)")

        block = ctx.enter_context(nc.Block())

        @block.sync
        def _(sp):
            sp.sem_inc(out_done, 16)
            for dst, src in (
                (cols[:, 0, :], pb), (cols[:, 1, :], norm_w), (cols[:, 2, :], norm_b), (cols[:, 3, :], bv1),
                (bq_c, bq1), (gamma_c, gamma), (eye[:], ident), (grp[:], group),
            ):
                sp.dma_start(dst, src).then_inc(consts_in, 16)
            sp.dma_start(by_partition(x_in[:]), wqk).then_inc(w_in, 16)
            sp.wait_ge(w_split, 1)
            for part, tile in enumerate((xh, xl)):
                sp.dma_start(
                    qk_hl[0:HEADS, :, part, :].rearrange("h p n -> p h n"),
                    by_partition(tile[:]).rearrange("p (h n) -> p h n", h=HEADS).bitcast(F32),
                ).then_inc(w_out, 16)
            sp.dma_start(by_partition(x_in[:, 0:2, :]), wv).then_inc(w_in, 16)
            sp.dma_start(by_partition(x_in[:, 2:4, :]), wv1).then_inc(w_in, 16)
            sp.wait_ge(w_split, 2)
            for part, tile in enumerate((xh, xl)):
                sp.dma_start(v_hl[:, part, :], by_partition(tile[:, 0:2, :]).bitcast(F32)).then_inc(w_out, 16)
                sp.dma_start(v1_hl[:, part, :], by_partition(tile[:, 2:4, :]).bitcast(F32)).then_inc(w_out, 16)
            sp.dma_start(by_partition(x_in[:, 0:2, :]), wp).then_inc(w_in, 16)
            sp.dma_start(x_in[:, 2, 0 : KT * P], wq1).then_inc(w_in, 16)
            sp.wait_ge(w_split, 3)
            for part, tile in enumerate((xh, xl)):
                sp.dma_start(
                    p_hl[:, :, part, :].rearrange("t p n -> p t n"),
                    by_partition(tile[:, 0:2, :]).rearrange("p (t n) -> p t n", t=KT).bitcast(F32),
                ).then_inc(w_out, 16)
                sp.dma_start(qk_hl[HEADS, :, part, :], tile[:, 2, 0 : KT * P].bitcast(F32)).then_inc(w_out, 16)
            sp.dma_start(x_in[:], x[0]).then_inc(x_loaded, 16)
            sp.wait_ge(w_out, 10 * 16)

            with sp.Fori(0, B) as b:
                following = sp.snap((b + 1) % B)

                def wait_filled(what):
                    sp.wait_ge(filled[pair_of(what)], filling(b, what))

                def load_wqk(h):
                    if h >= 2:
                        wait_filled(("qk", h - 2))
                    sp.dma_start(w_qk[h % 2][:].bitcast(F32), qk_hl[h].rearrange("p a (k n) -> p a k n", k=KT)).then_inc(
                        wqk_loaded[h % 2], 16
                    )

                def twins(h):
                    sp.wait_ge(qk_hi, b * HEADS + h + 1)
                    sp.dma_start(q_hh[h % 2][D:P, :].bitcast(F32), q_hh[h % 2][0:D, :].bitcast(F32)).then_inc(qk_twin[h % 2], 16)
                    sp.dma_start(k_hl[h % 2][0:D, :].bitcast(F32), k_h1[h % 2][0:D, :].bitcast(F32)).then_inc(qk_twin[h % 2], 16)

                sp.wait_ge(pv_done, 1 + b * TILES)
                sp.dma_start(w_v[:].bitcast(F32), v_hl.rearrange("p a (k n) -> p a k n", k=KT)).then_inc(wv_loaded, 16)
                load_wqk(0)
                load_wqk(1)
                sp.dma_start(w_p[:].bitcast(F32), p_hl[0]).then_inc(wp_loaded, 16)
                wait_filled(("v", ST - 1))
                wait_filled(("v", ST - 2))
                sp.dma_start(w_v[:].bitcast(F32), v1_hl.rearrange("p a (k n) -> p a k n", k=KT)).then_inc(wv_loaded, 16)
                twins(0)
                load_wqk(2)
                twins(1)
                load_wqk(3)

                def spread_denominators(h):
                    sp.wait_ge(drained["acc"], use(b, ("pv", h), done=1))
                    row = rows_of(h + 1).start
                    sp.dma_start(den_c[:], hf[row : row + 1, :]).then_inc(den_spread, 16)

                def return_inverses(h):
                    sp.wait_ge(rden_ready, b * HEADS + h + 1)
                    sp.dma_start(rden_row[h % 2].rearrange("(p c) -> p c", p=P), rden_c[:]).then_inc(rden_out, 16)
                    if h % 2 == 0 and h:
                        wait_filled(("proj", h // 2 - 1, KT - 1))
                        sp.dma_start(w_p[:].bitcast(F32), p_hl[h // 2]).then_inc(wp_loaded, 16)
                    sp.wait_ge(rden_out, 16 * (b * HEADS + h + 1))
                    sp.dma_start(
                        hl[rows_of(h), :].bitcast(F32), rden_row[h % 2 : h % 2 + 1, :].to_broadcast([D, N])
                    ).then_inc(rden_back, 16)

                for h in range(1, HEADS):
                    spread_denominators(h - 1)
                    if h + 1 < HEADS:
                        twins(h + 1)
                    if h + 3 <= HEADS:
                        load_wqk(h + 3)
                    return_inverses(h - 1)
                    if h == PROJ_HEADS[0]:
                        what = ("proj", 0, KT - 1)
                        sp.wait_ge(drained[pair_of(what)], use(b, what, done=1))
                        sp.dma_start(x_in[:], x[bass.ds(following, 1)].rearrange("b p k n -> (b p) k n")).then_inc(
                            x_loaded, 16
                        )
                spread_denominators(HEADS - 1)
                return_inverses(HEADS - 1)
                for n in range(NH):
                    sp.wait_ge(out_ready, b * NH + n + 1)
                    sp.dma_start(
                        out[bass.ds(b, 1)].rearrange("b p k n -> (b p) k n")[:, :, half(n)], x_mid[:, :, half(n)]
                    ).then_inc(out_done, 16)
            sp.wait_ge(x_loaded, (B + 1) * 16)
            sp.wait_ge(out_done, 16 + B * NH * 16)

        @block.gpsimd
        def _(pool):
            pool.sem_inc(h_lo, 1)
            nc.gpsimd.memset(minus_half, -0.5)
            nc.gpsimd.memset(ones[:].bitcast(F32), 1.0)
            nc.gpsimd.memset(k_h1[0][:].bitcast(F32), 1.0)
            nc.gpsimd.memset(k_h1[1][:].bitcast(F32), 1.0).then_inc(ones_set, 1)
            pool.wait_ge(ones_set, 1)
            with pool.Fori(0, B) as b:
                pool.wait_ge(pv_done, 1 + b * TILES)
                nc.gpsimd.tensor_tensor(unused, minus_half, minus_half, ALU.add)
                for j in range(ST):
                    nc.gpsimd.memset(vh[:, j, :, 1, :].bitcast(F32), 1.0)
                    last = nc.gpsimd.memset(vl[:, j, :, 1, :].bitcast(F32), 0.0)
                last.then_inc(ones_set, 1)
                pool.wait_ge(drained["acc"], use(b, ("var",), done=1))
                nc.gpsimd.tensor_tensor(rstd_c, var_c, minus_half, ALU.pow).then_inc(rstd_ready, 1)
                for h in range(HEADS):
                    pool.wait_ge(h_hi, b * HEADS + h + 1)
                    r = rows_of(h)
                    nc.gpsimd.tensor_tensor(hl[r, :], hf[r, :], hh[r, :].bitcast(F32), ALU.subtract).then_inc(h_lo, 1)
                    pool.wait_ge(h_lo, 1 + b * HEADS + h + 1)

        @block.scalar
        def _(act):
            act.sem_inc(t1_drained, 1)
            for r in range(3):
                act.wait_ge(w_in, 16 * (1, 3, 5)[r])
                if r:
                    act.wait_ge(w_out, 16 * (0, 2, 6)[r])
                cut = (slice(0, 4), slice(0, 4), slice(0, 2))[r]
                last = nc.scalar.activation(xh[:, cut, :], x_in[:, cut, :], ACT.Copy)
                if r == 2:
                    last = nc.scalar.activation(xh[:, 2, 0 : KT * P], x_in[:, 2, 0 : KT * P], ACT.Copy)
                last.then_inc(w_hi, 1)
            act.wait_ge(consts_in, 16 * 8)
            act.wait_ge(w_out, 10 * 16)

            with act.Fori(0, B) as b:

                def wait_filled(what, pair=None):
                    act.wait_ge(filled[pair or pair_of(what)], filling(b, what, pair))

                def exps(i, pair_drained, src, width, scale):
                    w = slice(0, width)
                    act.wait_ge(hi_done, 1 + b * TILES + max(i - 1, 0))
                    nc.scalar.activation(eh[i % 2][:, w], src, ACT.Exp, scale=scale).then_inc(e_hi, 1)
                    act.wait_ge(e_lo, 1 + b * TILES + i)
                    nc.scalar.activation(ef[:, w], src, ACT.Exp, scale=scale).then_inc(pair_drained, 1)

                def split_qk(h):
                    wait_filled(("qk", h))
                    nc.scalar.activation(q_hh[h % 2][0:D, :], bank["misc"][0:D, :], ACT.Copy)
                    nc.scalar.activation(k_h1[h % 2][0:D, :], bank["misc"][D:P, :], ACT.Copy).then_inc(qk_hi, 1)

                def max_row(h):
                    wait_filled(("row", h))
                    nc.scalar.activation(q_lm[h % 2][D : D + 1, :], bank["s0"][0:1, :], ACT.Copy, scale=-1.0).then_inc(
                        drained["s0"], 1
                    )

                def copy_head(h):
                    act.wait_ge(pv_done, 1 + b * TILES + (h + 1) * ST)
                    act.wait_ge(h_lo, 1 + b * HEADS + h)
                    nc.scalar.activation(hf[:], bank["acc"][:], ACT.Copy).then_inc(drained["acc"], 1)

                def head_hi(h):
                    act.wait_ge(h_scaled, b * HEADS + h + 1)
                    r = rows_of(h)
                    nc.scalar.activation(hh[r, :], hf[r, :], ACT.Copy).then_inc(h_hi, 1)

                for k in range(KT):
                    act.wait_ge(y_ready, b * KT + k + 1)
                    nc.scalar.activation(xh[:, k, :], x_mid[:, k, :], ACT.Identity, bias=nb_c[:, k : k + 1]).then_inc(
                        norm_hi, 1
                    )
                for j in range(ST):
                    wait_filled(("v", j))
                    nc.scalar.activation(
                        vh[:, j, :, 0:3:2, :],
                        bank[S[j % 2]][:, 0:C].rearrange("p (a c d) -> p a c d", c=2, d=D),
                        ACT.Copy,
                    ).then_inc(v_hi, 1)
                split_qk(0)
                split_qk(1)
                max_row(0)
                for h in range(HEADS):
                    for j in range(ST):
                        wait_filled(("s", h, j))
                        exps(h * ST + j, drained[S[j % 2]], bank[S[j % 2]][:], N, SCALE)
                        if j == 0 and 1 <= h < HEADS - 1:
                            split_qk(h + 1)
                        if h and j == SCALE_AT[(h - 1) % 2] + 1:
                            head_hi(h - 1)
                    if h + 1 < HEADS:
                        max_row(h + 1)
                    copy_head(h)
                head_hi(HEADS - 1)

                for m in range(KT):
                    what = ("proj", KT - 1, m)
                    act.wait_ge(drained[pair_of(what)], use(b, what, done=1))
                    nc.scalar.activation(xh[:, m, :], x_mid[:, m, :], ACT.Copy).then_inc(mid_hi, 1)
                wait_filled(("g",))
                for dst, r in ((q_hh[0], slice(0, P)), (k_h1[0], slice(0, D)), (k_hl[0], slice(0, D))):
                    last = nc.scalar.activation(dst[r, :], bank["acc"][r, :], ACT.Identity, bias=bq_c[r, :])
                last.then_inc(mid_hi, 1)
                for j in range(ST):
                    wait_filled(("v1", j))
                    nc.scalar.activation(
                        vh[:, j].rearrange("p a c d -> p (a c d)")[:, 0:C], bank[S[j % 2]][:, 0:C], ACT.Copy
                    ).then_inc(v_hi, 1)
                max_row(HEADS)
                for i in range(NH * ST):
                    act.wait_ge(t1_filled, b * NH * ST + i + 1)
                    exps(HEADS * ST + i, t1_drained, bank["s0"][:, half(i % 2)], HALF, 1.0)

        @block.vector
        def _(dve):
            dve.sem_inc(e_lo, 1)
            for n in drained:
                dve.sem_inc(drained[n], 1)
            for r in range(3):
                dve.wait_ge(w_hi, r + 1)
                if r:
                    dve.wait_ge(w_out, 16 * (0, 2, 6)[r])
                cut = (slice(0, 4), slice(0, 4), slice(0, 2))[r]
                last = nc.vector.tensor_tensor(
                    xl[:, cut, :], x_in[:, cut, :], xh[:, cut, :].bitcast(F32), ALU.subtract
                )
                if r == 2:
                    w = slice(0, KT * P)
                    last = nc.vector.tensor_tensor(xl[:, 2, w], x_in[:, 2, w], xh[:, 2, w].bitcast(F32), ALU.subtract)
                last.then_inc(w_split, 1)
            dve.wait_ge(consts_in, 16 * 8)
            nc.vector.tensor_scalar(gb_c, bv_c, gamma_c, None, ALU.mult).then_inc(dve_step, 1)
            dve.wait_ge(dve_step, 1)
            dve.wait_ge(w_out, 10 * 16)

            with dve.Fori(0, B) as b:
                steps = [0]

                def link(ins):
                    ins.then_inc(dve_step, 1)
                    steps[0] += 1
                    dve.wait_ge(dve_step, b * DVE_LINKS + 1 + steps[0])

                def wait_filled(what, pair=None):
                    dve.wait_ge(filled[pair or pair_of(what)], filling(b, what, pair))

                def drain(ins, what, pair=None):
                    ins.then_inc(drained[pair or pair_of(what)], 1)

                def exp_lo(i, pair_drained, done, width):
                    w = slice(0, width)
                    dve.wait_ge(pair_drained, done)
                    dve.wait_ge(pv_done, 1 + b * TILES + max(i - 1, 0))
                    nc.vector.tensor_tensor(
                        el[i % 2][:, w], ef[:, w], eh[i % 2][:, w].bitcast(F32), ALU.subtract
                    ).then_inc(e_lo, 1)

                def row_max(h, t):
                    what = ("max", h, t)
                    wait_filled(what)
                    drain(nc.vector.reduce_max(mx[h % 2][:, t : t + 1], bank[pair_of(what)][:], AX_X), what)

                def add_proj(p, m):
                    what = ("proj", p, m)
                    wait_filled(what)
                    ps = bank[pair_of(what)]
                    if p == 0:
                        ins = nc.vector.scalar_tensor_tensor(
                            out=x_mid[:, m, :], in0=ps[:], scalar=pb_c[:, m : m + 1], in1=x_in[:, m, :],
                            op0=ALU.add, op1=ALU.add,
                        )
                    else:
                        ins = nc.vector.tensor_tensor(x_mid[:, m, :], ps[:], x_mid[:, m, :], ALU.add)
                    drain(ins, what)

                def lo_qk(h):
                    ps = bank["misc"]
                    dve.wait_ge(qk_hi, b * HEADS + h + 1)
                    s = h % 2
                    nc.vector.tensor_tensor(q_lm[s][0:D, :], ps[0:D, :], q_hh[s][0:D, :].bitcast(F32), ALU.subtract)
                    drain(
                        nc.vector.tensor_tensor(k_hl[s][D:P, :], ps[D:P, :], k_h1[s][0:D, :].bitcast(F32), ALU.subtract),
                        ("qk", h),
                    )

                def invert_denominators(h):
                    dve.wait_ge(den_spread, 16 * (b * HEADS + h + 1))
                    nc.vector.reciprocal(rden_c[:], den_c[:]).then_inc(rden_ready, 1)

                def scale_head(h):
                    dve.wait_ge(rden_back, 16 * (b * HEADS + h + 1))
                    r = rows_of(h)
                    nc.vector.tensor_tensor(hf[r, :], hf[r, :], hl[r, :].bitcast(F32), ALU.mult).then_inc(h_scaled, 1)

                dve.wait_ge(x_loaded, b * 16 + 16)
                for k in range(KT):
                    for n in range(NH):
                        last = nc.vector.bn_stats(stats[:, k, n, :], x_in[:, k, half(n)])
                link(last)
                nc.vector.memset(dev_c, 0.0)
                for k in range(KT):
                    last = nc.vector.bn_aggr(mv[:, k, :], stats[:, k, :, :])
                last.then_inc(stat_ready, 1)
                dve.wait_ge(stat_ready, b * 2 + 1)
                wait_filled(("mean",))
                drain(nc.vector.tensor_copy(mean_c, bank["acc"][:, 0:KT]), ("mean",))
                dve.wait_ge(drained["acc"], use(b, ("mean",), done=1))
                link(nc.vector.tensor_tensor(dev_c, mv[:, :, 0], mean_c, ALU.subtract))
                link(nc.vector.tensor_tensor(dev_c, dev_c, dev_c, ALU.mult))
                nc.vector.tensor_tensor(dev_c, dev_c, mv[:, :, 1], ALU.add).then_inc(stat_ready, 1)
                wait_filled(("var",))
                drain(nc.vector.tensor_scalar(var_c, bank["acc"][:, 0:KT], EPS, None, ALU.add), ("var",))
                dve.wait_ge(rstd_ready, b + 1)
                link(nc.vector.tensor_tensor(fac_c, rstd_c, nw_c, ALU.mult))
                dve.wait_ge(out_done, 16 + b * NH * 16)
                for k in range(KT):
                    c = slice(k, k + 1)
                    nc.vector.tensor_scalar(
                        x_mid[:, k, :], x_in[:, k, :], mean_c[:, c], fac_c[:, c], ALU.subtract, ALU.mult
                    ).then_inc(y_ready, 1)
                for k in range(KT):
                    dve.wait_ge(norm_hi, b * KT + k + 1)
                    nc.vector.scalar_tensor_tensor(
                        out=xl[:, k, :], in0=x_mid[:, k, :], scalar=nb_c[:, k : k + 1],
                        in1=xh[:, k, :].bitcast(F32), op0=ALU.add, op1=ALU.subtract,
                    ).then_inc(norm_lo, 1)

                for j in range(ST):
                    dve.wait_ge(v_hi, b * 2 * ST + j + 1)
                    drain(
                        nc.vector.tensor_tensor(
                            vl[:, j, :, 0:3:2, :],
                            bank[S[j % 2]][:, 0:C].rearrange("p (a c d) -> p a c d", c=2, d=D),
                            vh[:, j, :, 0:3:2, :].bitcast(F32),
                            ALU.subtract,
                        ),
                        ("v", j),
                    )
                lo_qk(0)
                lo_qk(1)
                for t in range(ST):
                    row_max(0, t)
                for h in range(HEADS):
                    for j in range(ST):
                        exp_lo(h * ST + j, drained[S[j % 2]], use(b, ("s", h, j), done=1), N)
                        if j == 0 and 1 <= h < HEADS - 1:
                            lo_qk(h + 1)
                        if h and j == 2:
                            invert_denominators(h - 1)
                        if h and j == SCALE_AT[(h - 1) % 2]:
                            scale_head(h - 1)
                        if h + 1 < HEADS and j in MAX_BETWEEN:
                            row_max(h + 1, MAX_BETWEEN[j])
                        if h in PROJ_HEADS and j in PROJ_BETWEEN:
                            add_proj(h // 2 - 1, PROJ_BETWEEN[j])
                        if h + 1 < HEADS and j in MAX_AFTER:
                            row_max(h + 1, MAX_AFTER[j])
                invert_denominators(HEADS - 1)
                scale_head(HEADS - 1)

                for m in range(KT):
                    add_proj(KT - 1, m)
                for m in range(KT):
                    dve.wait_ge(mid_hi, b * (KT + 1) + m + 1)
                    nc.vector.tensor_tensor(
                        xl[:, m, :], x_mid[:, m, :], xh[:, m, :].bitcast(F32), ALU.subtract
                    ).then_inc(mid_lo, 1)
                dve.wait_ge(mid_hi, b * (KT + 1) + KT + 1)
                for dst, r in ((q_lm[0], slice(0, D)), (k_hl[0], slice(D, P))):
                    last = nc.vector.scalar_tensor_tensor(
                        out=dst[r, :], in0=bank["acc"][r, :], scalar=bq_c[r, :], in1=q_hh[0][r, :].bitcast(F32),
                        op0=ALU.add, op1=ALU.subtract,
                    )
                drain(last, ("g",))
                for j in range(ST):
                    dve.wait_ge(v_hi, b * 2 * ST + ST + j + 1)
                    v_of = [t[:, j].rearrange("p a c d -> p (a c d)")[:, 0:C] for t in (vl, vh)]
                    drain(
                        nc.vector.tensor_tensor(v_of[0], bank[S[j % 2]][:, 0:C], v_of[1].bitcast(F32), ALU.subtract),
                        ("v1", j),
                    )
                for t in range(ST):
                    row_max(HEADS, t)
                for n in range(NH):
                    for j in range(ST):
                        i = n * ST + j
                        exp_lo(HEADS * ST + i, t1_drained, 1 + b * NH * ST + i + 1, HALF)
                    wait_filled(("den", n))
                    dve.wait_ge(h_lo, 1 + (b + 1) * HEADS)
                    rden, scaled = hf[:, half(0)], hf[:, half(1)]
                    drain(nc.vector.reciprocal(rden, bank["s1"][:, half(0)]), ("den", n))
                    dve.wait_ge(drained["s1"], use(b, ("den", n), done=1))
                    link(nc.vector.tensor_scalar(rden, rden, gamma_c, None, ALU.mult))
                    for m in range(KT):
                        pair = ("acc", "misc")[m // 2]
                        if m == 0:
                            wait_filled(("o", n), pair)
                        if m == 2:
                            dve.wait_ge(pv_done, 1 + b * TILES + (HEADS + n + 1) * ST)
                        ins = nc.vector.tensor_tensor(scaled, bank[pair][:, half(m % 2)], rden, ALU.mult)
                        if m % 2:
                            drain(ins, ("o", n), pair)
                            dve.wait_ge(drained[pair], use(b, ("o", n), pair, done=1))
                        else:
                            link(ins)
                        last = nc.vector.scalar_tensor_tensor(
                            out=x_mid[:, m, half(n)], in0=scaled, scalar=gb_c[:, m : m + 1],
                            in1=x_mid[:, m, half(n)], op0=ALU.add, op1=ALU.add,
                        )
                        if m < KT - 1:
                            link(last)
                    last.then_inc(out_ready, 1)
                    dve.wait_ge(out_ready, b * NH + n + 1)
                assert steps[0] == DVE_LINKS, steps

        @block.tensor
        def _(pe):
            pe.sem_inc(hi_done, 1)
            pe.sem_inc(pv_done, 1)
            pe.wait_ge(consts_in, 16 * 8)
            pe.wait_ge(ones_set, 1)
            with pe.Fori(0, B) as b:

                def wait_free(what, pair=None):
                    pe.wait_ge(drained[pair or pair_of(what)], use(b, what, pair))

                def fill(ins, what, pair=None):
                    ins.then_inc(filled[pair or pair_of(what)], 1)

                def product(ps, hi_lo_pairs):
                    n = len(hi_lo_pairs)
                    for k, ((wh_, wl_), (mh, ml)) in enumerate(hi_lo_pairs):
                        nc.tensor.matmul(ps, wh_, mh, start=k == 0, stop=False)
                        nc.tensor.matmul(ps, wh_, ml, start=False, stop=False)
                        last = nc.tensor.matmul(ps, wl_, mh, start=False, stop=k == n - 1)
                    return last

                def project_v(j, what):
                    wait_free(what)
                    t = slice(j * P, (j + 1) * P)
                    fill(
                        product(
                            bank[pair_of(what)][:, 0:C],
                            [((xh[:, k, t], xl[:, k, t]), (w_v[:, 0, k, :], w_v[:, 1, k, :])) for k in range(KT)],
                        ),
                        what,
                    )

                def project_qk(w, what, n):
                    last = product(
                        bank[pair_of(what)][:, half(n)],
                        [((w[:, 0, k, :], w[:, 1, k, :]), (xh[:, k, half(n)], xl[:, k, half(n)])) for k in range(KT)],
                    )
                    if n == NH - 1:
                        fill(last, what)

                def qk_half(h, n):
                    if n == 0:
                        wait_free(("qk", h))
                        loads = HEADS // 2 + 1 - h % 2
                        pe.wait_ge(wqk_loaded[h % 2], 16 * (b * loads + h // 2 + 1))
                    project_qk(w_qk[h % 2], ("qk", h), n)

                def max_tile(h, t):
                    what = ("max", h, t)
                    wait_free(what)
                    for n in range(NH):
                        last = nc.tensor.matmul(
                            bank[pair_of(what)][:, half(n)], q_hh[h % 2][0:D, t * P : (t + 1) * P],
                            k_h1[h % 2][0:D, half(n)], start=True, stop=True,
                        )
                    fill(last, what)

                def max_row(h):
                    for p in ("misc", "acc") if h in (0, HEADS) else ("misc",):
                        t = max(t for t in range(ST) if ("max", h, t) in USES[p])
                        pe.wait_ge(drained[p], use(b, ("max", h, t), done=1))
                    wait_free(("row", h))
                    for t in range(ST):
                        last = nc.tensor.transpose(
                            bank["s0"][0:1, t * P : (t + 1) * P], mx[h % 2][:, t : t + 1], eye[:]
                        )
                    fill(last, ("row", h))

                def scores(s, ps, j, n):
                    keys = slice(j * P, (j + 1) * P)
                    nc.tensor.matmul(ps, k_hl[s][:, keys], q_hh[s][:, half(n)], start=True, stop=False)
                    return nc.tensor.matmul(
                        ps, k_h1[s][0 : D + 1, keys], q_lm[s][0 : D + 1, half(n)], start=False, stop=True
                    )

                def head_scores(h, j):
                    what = ("s", h, j)
                    wait_free(what)
                    if j == 0:
                        pe.wait_ge(qk_twin[h % 2], 32 * (b * (HEADS // 2) + h // 2 + 1))
                        pe.wait_ge(drained["misc"], use(b, ("qk", h), done=1))
                    for n in range(NH):
                        last = scores(h % 2, bank[S[j % 2]][:, half(n)], j, n)
                    fill(last, what)

                def head_pv_hi(h, j):
                    i = h * ST + j
                    if j == 0:
                        wait_free(("pv", h))
                    pe.wait_ge(e_hi, b * TILES + i + 1)
                    for n in range(NH):
                        ps, moving = bank["acc"][:, half(n)], eh[i % 2][:, half(n)]
                        nc.tensor.matmul(ps, head_v(vh, h, j), moving, start=j == 0, stop=False)
                        last = nc.tensor.matmul(ps, head_v(vl, h, j), moving, start=False, stop=False)
                    last.then_inc(hi_done, 1)

                def head_pv_lo(h, j):
                    i = h * ST + j
                    pe.wait_ge(e_lo, 1 + b * TILES + i + 1)
                    for n in range(NH):
                        last = nc.tensor.matmul(
                            bank["acc"][:, half(n)], head_v(vh, h, j), el[i % 2][:, half(n)],
                            start=False, stop=j == ST - 1,
                        )
                    last.then_inc(pv_done, 1)

                def project_out(p, m):
                    what = ("proj", p, m)
                    wait_free(what)
                    if m == 0:
                        pe.wait_ge(wp_loaded, 16 * (b * KT + p + 1))
                        pe.wait_ge(h_lo, 1 + b * HEADS + 2 * p + 2)
                    c = slice(m * P, (m + 1) * P)
                    for n in range(NH):
                        last = product(
                            bank[pair_of(what)][:, half(n)],
                            [((w_p[:, 0, c], w_p[:, 1, c]), (hh[:, half(n)], hl[:, half(n)]))],
                        )
                    fill(last, what)

                pe.wait_ge(stat_ready, b * 2 + 1)
                wait_free(("mean",))
                fill(nc.tensor.matmul(bank["acc"][:, 0:KT], grp[:], mv[:, :, 0], start=True, stop=True), ("mean",))
                pe.wait_ge(stat_ready, b * 2 + 2)
                wait_free(("var",))
                fill(nc.tensor.matmul(bank["acc"][:, 0:KT], grp[:], dev_c, start=True, stop=True), ("var",))

                pe.wait_ge(norm_lo, (b + 1) * KT)
                pe.wait_ge(wv_loaded, 16 * (2 * b + 1))
                pe.wait_ge(t1_drained, 1 + b * NH * ST)
                for j in range(ST):
                    project_v(j, ("v", j))
                for h in range(2):
                    for n in range(NH):
                        qk_half(h, n)
                pe.wait_ge(drained["misc"], use(b, ("qk", 0), done=1))
                for t in range(ST):
                    max_tile(0, t)
                max_row(0)
                pe.wait_ge(ones_set, b + 2)
                head_scores(0, 0)
                for h in range(HEADS):
                    for j in range(ST):
                        if j + 1 < ST:
                            head_scores(h, j + 1)
                        if h + 1 < HEADS and j in MAX_BETWEEN:
                            max_tile(h + 1, MAX_BETWEEN[j])
                        if h in PROJ_HEADS and j in PROJ_BETWEEN:
                            project_out(h // 2 - 1, PROJ_BETWEEN[j])
                        head_pv_hi(h, j)
                        if j:
                            head_pv_lo(h, j - 1)
                        if h + 1 < HEADS and j in MAX_AFTER:
                            max_tile(h + 1, MAX_AFTER[j])
                    if h + 1 < HEADS:
                        max_row(h + 1)
                    if h + 2 < HEADS:
                        qk_half(h + 2, 0)
                    head_pv_lo(h, ST - 1)
                    if h + 1 < HEADS:
                        head_scores(h + 1, 0)
                    if h + 2 < HEADS:
                        qk_half(h + 2, 1)

                for m in range(KT):
                    project_out(KT - 1, m)

                pe.wait_ge(mid_lo, (b + 1) * KT)
                pe.wait_ge(wqk_loaded[0], 16 * (b + 1) * (HEADS // 2 + 1))
                wait_free(("g",))
                for n in range(NH):
                    project_qk(w_qk[0], ("g",), n)
                pe.wait_ge(wv_loaded, 16 * (2 * b + 2))
                for j in range(ST):
                    project_v(j, ("v1", j))
                pe.wait_ge(drained["acc"], use(b, ("g",), done=1))
                for t in range(ST):
                    max_tile(HEADS, t)
                max_row(HEADS)

                def scores1(i):
                    n, j = divmod(i, ST)
                    if i == 0:
                        pe.wait_ge(drained["s0"], use(b, ("row", HEADS), done=1))
                    pe.wait_ge(t1_drained, 1 + b * NH * ST + max(i - 1, 0))
                    scores(0, bank["s0"][:, half(i % 2)], j, n).then_inc(t1_filled, 1)

                den = bank["s1"][:, half(0)]

                def out_of(m):
                    return bank[("acc", "misc")[m // 2]][:, half(m % 2)]

                def v1_of(tile, j, m):
                    return tile[:, j].rearrange("p a c d -> p (a c d)")[:, m * P : (m + 1) * P]

                def pv_hi1(n, j):
                    i = HEADS * ST + n * ST + j
                    if j == 0:
                        wait_free(("o", n), "acc")
                        wait_free(("o", n), "misc")
                        wait_free(("den", n))
                    pe.wait_ge(e_hi, b * TILES + i + 1)
                    moving = eh[i % 2][:, 0:HALF]
                    nc.tensor.matmul(den, ones[:], moving, start=j == 0, stop=False)
                    for m in range(KT):
                        nc.tensor.matmul(out_of(m), v1_of(vh, j, m), moving, start=j == 0, stop=False)
                        last = nc.tensor.matmul(out_of(m), v1_of(vl, j, m), moving, start=False, stop=False)
                    last.then_inc(hi_done, 1)

                def pv_lo1(n, j):
                    i = HEADS * ST + n * ST + j
                    end = j == ST - 1
                    pe.wait_ge(e_lo, 1 + b * TILES + i + 1)
                    moving = el[i % 2][:, 0:HALF]
                    last = nc.tensor.matmul(den, ones[:], moving, start=False, stop=end)
                    if end:
                        fill(last, ("den", n))
                    for m in range(KT):
                        last = nc.tensor.matmul(out_of(m), v1_of(vh, j, m), moving, start=False, stop=end)
                        if end and m == 1:
                            fill(last, ("o", n), "acc")
                    last.then_inc(pv_done, 1)

                scores1(0)
                for n in range(NH):
                    for j in range(ST):
                        if n * ST + j + 1 < NH * ST:
                            scores1(n * ST + j + 1)
                        pv_hi1(n, j)
                        if j:
                            pv_lo1(n, j - 1)
                    pv_lo1(n, ST - 1)


def kernel(x, L0_conv_norm_w, L0_conv_norm_b, L0_conv_qkv_w, L0_conv_proj_w, L0_conv_proj_b, L1_conv_Wq, L1_conv_bq, L1_conv_Wv, L1_conv_bv, L1_conv_gamma):
    import concourse.bacc as bacc
    from concourse.bass_utils import run_bass_kernel_spmd

    def array(a):
        return np.ascontiguousarray(np.asarray(a))

    def by_channel(v):
        return array(v).reshape(KT, P).T

    def stationary(w):
        return array(w).reshape(-1, KT, P).transpose(2, 1, 0)

    qkv = array(L0_conv_qkv_w).reshape(HEADS, 3 * D, C)
    arrays = {
        "x": array(x).reshape(B, C, N),
        "wqk": qkv[:, 0 : 2 * D].reshape(HEADS, 2 * D, KT, P).transpose(3, 0, 2, 1).reshape(P, -1),
        "wv": stationary(qkv[:, 2 * D :].reshape(C, C)).reshape(P, -1),
        "wv1": stationary(L1_conv_Wv).reshape(P, -1),
        "wp": stationary(L0_conv_proj_w).reshape(P, -1),
        "wq1": stationary(np.concatenate([array(L1_conv_Wq)] * 2)).reshape(P, -1),
        "pb": by_channel(L0_conv_proj_b),
        "norm_w": by_channel(L0_conv_norm_w),
        "norm_b": by_channel(L0_conv_norm_b),
        "bv1": by_channel(L1_conv_bv),
        "bq1": np.concatenate([array(L1_conv_bq)] * 2).reshape(P, 1),
        "gamma": np.repeat(array(L1_conv_gamma), P).reshape(P, 1),
        "group": np.kron(np.eye(P * GROUPS // C), np.full((C // GROUPS,) * 2, GROUPS / C)).astype(np.float32),
        "ident": np.eye(P, dtype=np.float32),
    }
    nc = bacc.Bacc("TRN2", target_bir_lowering=False, num_devices=1)
    arrays = {f"in_{n}": array(a) for n, a in arrays.items()}
    aps = [nc.dram_tensor(n, a.shape, F32, kind="ExternalInput").ap() for n, a in arrays.items()]
    out = nc.dram_tensor("out", (B, C, N), F32, kind="ExternalOutput").ap()
    aps[0], out = (a.rearrange("b (k p) n -> b p k n", p=P) for a in (aps[0], out))
    attention_kernel(nc, *aps, out)
    result = run_bass_kernel_spmd(nc, [arrays], core_ids=[0])
    return result.results[0]["out"].reshape(np.shape(x))
```

```python
from contextlib import ExitStack

import numpy as np

import concourse.bass as bass
from concourse import mybir

B, C, N = 8, 512, 1024
P = 128
KT = C // P
ST = N // P
HEADS = 8
D = C // HEADS
HALF = 512
NH = N // HALF
GROUPS = 32
EPS = 1e-5
SCALE = float(D) ** -0.5

F32 = mybir.dt.float32
F32R = mybir.dt.float32r
ALU = mybir.AluOpType
ACT = mybir.ActivationFunctionType
AX_X = mybir.AxisListType.X

MAX_BETWEEN = {3: 2, 6: 6}
MAX_AFTER = {1: 0, 2: 1, 3: 3, 4: 4, 5: 5, 6: 7}
PROJ_BETWEEN = {1: 0, 2: 1, 4: 2, 5: 3}
PROJ_HEADS = (3, 5, 7)
SCALE_AT = {1: 4, 0: 6}


MAX_WITH_V = {3: (0, 1), 4: (2, 3), 5: (4, 5), 6: (6, 7)}
STATS_AT = {j: (j // NH, j % NH) for j in range(ST)}
MEAN_AT, VAR_AT = 0, 1
NORM_Y = {3: (0, 1), 4: (2, 3)}
NORM_HI = {4: (0,), 5: (1, 2), 6: (3,)}
NORM_LO = {5: (0,), 6: (1, 2), 7: (3,)}
OUTPUT_AT = {1: (), 2: (0,), 3: (1,), 4: (2,), 5: (3,)}
LAST = KT - 1


def psum_uses():
    start = {"s0": [], "s1": [("mean",), ("var",)], "acc": [], "misc": []}
    s0, s1, acc, misc = [], [], [], []
    misc += [("qk", 0)]
    for j in range(ST):
        (s0, s1)[j % 2].append(("v", j))
        for t in MAX_WITH_V.get(j, ()):
            (misc, acc)[t % 2].append(("max", 0, t))
    s0.append(("row", 0))
    misc += [("qk", 1)]
    for h in range(HEADS):
        acc.append(("pv", h))
        for j in range(ST):
            (s0, s1)[j % 2].append(("s", h, j))
            if h + 1 < HEADS and j in MAX_BETWEEN:
                misc.append(("max", h + 1, MAX_BETWEEN[j]))
            if h in PROJ_HEADS and j in PROJ_BETWEEN:
                misc.append(("proj", h // 2 - 1, PROJ_BETWEEN[j]))
            if h + 1 < HEADS and j in MAX_AFTER:
                misc.append(("max", h + 1, MAX_AFTER[j]))
        if h + 1 < HEADS:
            s0.append(("row", h + 1))
        if h + 2 < HEADS:
            misc.append(("qk", h + 2))
    for n in range(NH):
        for m in range(KT):
            (misc, s0, s1, acc)[m].append(("proj", LAST, m, n))
    misc += [("g", n) for n in range(NH)]
    for j in range(ST):
        (s0, s1)[j % 2].append(("v1", j))
        for t in MAX_WITH_V.get(j, ()):
            (misc, acc)[t % 2].append(("max", HEADS, t))
    s0.append(("row", HEADS))
    s1 += [("mean",), ("var",)]
    for n in range(NH):
        s1.append(("den", n))
        acc.append(("o", n))
        misc.append(("o", n))
    return start, {"s0": s0, "s1": s1, "acc": acc, "misc": misc}


START, USES = psum_uses()
TILES = HEADS * ST + NH * ST
START_LINKS = 5
DVE_LINKS = 6 + 6 * NH


def pair_of(what):
    return next(pair for pair in USES if what in USES[pair])


def slot_of(h):
    return 1 if h == HEADS else h % 2


def filling(b, what, pair=None):
    pair = pair or pair_of(what)
    if b is None:
        return START[pair].index(what) + 1
    signalled = [w for w in USES[pair] if not on_pv_done(w, pair)]
    return len(START[pair]) + b * len(signalled) + signalled.index(what) + 1


def on_pv_done(what, pair):
    return what[0] == "pv" or (what[0] == "o" and pair == "misc")


def use(b, what, pair=None, done=0):
    pair = pair or pair_of(what)
    if b is None:
        return 1 + START[pair].index(what) + done
    return 1 + len(START[pair]) + b * len(USES[pair]) + USES[pair].index(what) + done


def attention_kernel(nc, x, wqk, wv, wv1, wp, wq1, pb, norm_w, norm_b, bv1, bq1, gamma, group, ident, out):
    with ExitStack() as ctx:
        def sb(name, shape, dt=F32):
            return ctx.enter_context(nc.sbuf_tensor(name, shape, dt))

        def sem(name):
            return ctx.enter_context(nc.semaphore(name))

        qk_hl = nc.dram_tensor("qk_hl", [HEADS + 1, P, 2, KT * P], F32, kind="Internal").ap()
        v_hl = nc.dram_tensor("v_hl", [P, 2, KT * C], F32, kind="Internal").ap()
        v1_hl = nc.dram_tensor("v1_hl", [P, 2, KT * C], F32, kind="Internal").ap()
        p_hl = nc.dram_tensor("p_hl", [KT, P, 2, C], F32, kind="Internal").ap()

        rden_row = nc.dram_tensor("rden_row", [2, N], F32, kind="Internal").ap()

        with ExitStack() as shared:
            hh_f, hl_f, wp_f = (shared.enter_context(nc.sbuf_tensor(n, [P, N], F32)) for n in ("hh_f", "hl_f", "wp_f"))
        hh = sb("hh", [P, N], F32R)
        hl = sb("hl", [P, N], F32R)
        w_p = sb("w_p", [P, 2, C], F32R)
        x_in = sb("x_in", [P, KT, N])
        x_mid = sb("x_mid", [P, KT, N])
        xh = sb("xh", [P, KT, N], F32R)
        xl = sb("xl", [P, KT, N], F32R)
        w_qk = [sb(f"w_qk{i}", [P, 2, KT, P], F32R) for i in range(2)]
        w_v = sb("w_v", [P, 2, KT, C], F32R)
        k_hl = [sb(f"k_hl{i}", [P, N], F32R) for i in range(2)]
        q_hh = [sb(f"q_hh{i}", [P, N], F32R) for i in range(2)]
        k_h1 = [sb(f"k_h1{i}", [P, N], F32R) for i in range(2)]
        q_lm = [sb(f"q_lm{i}", [P, N], F32R) for i in range(2)]
        vh = sb("vh", [P, ST, HEADS // 2, 3, D], F32R)
        vl = sb("vl", [P, ST, HEADS // 2, 3, D], F32R)
        ef = sb("ef", [P, N])
        eh = [sb(f"eh{i}", [P, N], F32R) for i in range(2)]
        el = [sb(f"el{i}", [P, N], F32R) for i in range(2)]
        hf = sb("hf", [P, N])
        den_c, rden_c = sb("den_c", [P, N // P]), sb("rden_c", [P, N // P])
        ones = sb("ones", [P, P], F32R)
        eye = sb("eye", [P, P])
        grp = sb("grp", [P, P])
        mx = [sb(f"mx{i}", [P, ST]) for i in range(2)]
        cols = sb("cols", [P, 5, KT])
        pb_c, nw_c, nb_c, bv_c, gb_c = (cols[:, i, :] for i in range(5))
        scal = sb("scal", [P, 2])
        bq_c, gamma_c = scal[:, 0:1], scal[:, 1:2]
        stats = sb("stats", [P, KT, NH, 6])
        mv = sb("mv", [P, KT, 2])
        gm = sb("gm", [P, 7, KT])
        mean_c, dev_c, var_c, rstd_c, fac_c, minus_half, unused = (gm[:, i, :] for i in range(7))

        bank = {n: ctx.enter_context(nc.psum_tensor(f"ps_{n}", [P, N], F32)) for n in USES}
        S = ("s0", "s1")

        filled = {n: sem(f"{n}_filled") for n in bank}
        drained = {n: sem(f"{n}_drained") for n in bank}
        w_in, w_hi, w_split, w_out = sem("w_in"), sem("w_hi"), sem("w_split"), sem("w_out")
        consts_in, ones_set, x_loaded = sem("consts_in"), sem("ones_set"), sem("x_loaded")
        stat_ready, rstd_ready, y_ready = sem("stat_ready"), sem("rstd_ready"), sem("y_ready")
        norm_hi, norm_lo = sem("norm_hi"), sem("norm_lo")
        g_hi, tail_hi, tail_lo = sem("g_hi"), sem("tail_hi"), sem("tail_lo")
        v_hi, mid_hi, mid_lo = sem("v_hi"), sem("mid_hi"), sem("mid_lo")
        wqk_loaded = [sem(f"wqk_loaded{i}") for i in range(2)]
        wv_loaded, wp_loaded = sem("wv_loaded"), sem("wp_loaded")
        qk_hi, qk_twin = sem("qk_hi"), [sem(f"qk_twin{i}") for i in range(2)]
        e_hi, e_lo, hi_done, pv_done = sem("e_hi"), sem("e_lo"), sem("hi_done"), sem("pv_done")
        h_hi, h_lo, h_scaled = sem("h_hi"), sem("h_lo"), sem("h_scaled")
        den_spread, rden_ready, rden_out, rden_back = (
            sem(n) for n in ("den_spread", "rden_ready", "rden_out", "rden_back")
        )
        t1_filled, t1_drained = sem("t1_filled"), sem("t1_drained")
        out_ready, out_done, dve_step = sem("out_ready"), sem("out_done"), sem("dve_step")

        def head_v(tile, h, j):
            start = (h // 2) * 3 * D + (h % 2) * D
            return tile[:, j].rearrange("p a c d -> p (a c d)")[:, start : start + P]

        def rows_of(h):
            return slice(D * (h % 2), D * (h % 2) + D)

        def half(n):
            return slice(n * HALF, (n + 1) * HALF)

        y_of = [hf[:], hh_f[:], hl_f[:], wp_f[:]]
        outs = [t[:, half(i)] for t in (hh_f, hl_f) for i in range(NH)]

        def by_partition(w):
            return w.rearrange("p k n -> p (k n)")

        block = ctx.enter_context(nc.Block())

        @block.sync
        def _(sp):
            sp.sem_inc(out_done, 16)
            for dst, src in (
                (cols[:, 0, :], pb), (cols[:, 1, :], norm_w), (cols[:, 2, :], norm_b), (cols[:, 3, :], bv1),
                (bq_c, bq1), (gamma_c, gamma), (eye[:], ident), (grp[:], group),
            ):
                sp.dma_start(dst, src).then_inc(consts_in, 16)
            sp.dma_start(by_partition(x_in[:]), wqk).then_inc(w_in, 16)
            sp.wait_ge(w_split, 1)
            for part, tile in enumerate((xh, xl)):
                sp.dma_start(
                    qk_hl[0:HEADS, :, part, :].rearrange("h p n -> p h n"),
                    by_partition(tile[:]).rearrange("p (h n) -> p h n", h=HEADS).bitcast(F32),
                ).then_inc(w_out, 16)
            sp.dma_start(by_partition(x_in[:, 0:2, :]), wv).then_inc(w_in, 16)
            sp.dma_start(by_partition(x_in[:, 2:4, :]), wv1).then_inc(w_in, 16)
            sp.wait_ge(w_split, 2)
            for part, tile in enumerate((xh, xl)):
                sp.dma_start(v_hl[:, part, :], by_partition(tile[:, 0:2, :]).bitcast(F32)).then_inc(w_out, 16)
                sp.dma_start(v1_hl[:, part, :], by_partition(tile[:, 2:4, :]).bitcast(F32)).then_inc(w_out, 16)
            sp.dma_start(by_partition(x_in[:, 0:2, :]), wp).then_inc(w_in, 16)
            sp.dma_start(x_in[:, 2, 0 : KT * P], wq1).then_inc(w_in, 16)
            sp.wait_ge(w_split, 3)
            for part, tile in enumerate((xh, xl)):
                sp.dma_start(
                    p_hl[:, :, part, :].rearrange("t p n -> p t n"),
                    by_partition(tile[:, 0:2, :]).rearrange("p (t n) -> p t n", t=KT).bitcast(F32),
                ).then_inc(w_out, 16)
                sp.dma_start(qk_hl[HEADS, :, part, :], tile[:, 2, 0 : KT * P].bitcast(F32)).then_inc(w_out, 16)
            sp.dma_start(x_in[:], x[0]).then_inc(x_loaded, 16)
            sp.wait_ge(w_out, 10 * 16)
            sp.dma_start(w_qk[0][:].bitcast(F32), qk_hl[0].rearrange("p a (k n) -> p a k n", k=KT)).then_inc(wqk_loaded[0], 16)
            sp.dma_start(w_v[:].bitcast(F32), v_hl.rearrange("p a (k n) -> p a k n", k=KT)).then_inc(wv_loaded, 16)

            with sp.Fori(0, B) as b:
                following = sp.snap((b + 1) % B)

                def wait_filled(what):
                    sp.wait_ge(filled[pair_of(what)], filling(b, what))

                def load_wqk(h, after):
                    s = slot_of(h)
                    wait_filled(after)
                    sp.dma_start(w_qk[s][:].bitcast(F32), qk_hl[h].rearrange("p a (k n) -> p a k n", k=KT)).then_inc(
                        wqk_loaded[s], 16
                    )

                def twins(h):
                    sp.wait_ge(qk_hi, b * HEADS + h + 1)
                    sp.dma_start(q_hh[h % 2][D:P, :].bitcast(F32), q_hh[h % 2][0:D, :].bitcast(F32)).then_inc(qk_twin[h % 2], 16)
                    sp.dma_start(k_hl[h % 2][0:D, :].bitcast(F32), k_h1[h % 2][0:D, :].bitcast(F32)).then_inc(qk_twin[h % 2], 16)

                sp.wait_ge(norm_lo, (b + 1) * KT)
                sp.dma_start(w_qk[1][:].bitcast(F32), qk_hl[1].rearrange("p a (k n) -> p a k n", k=KT)).then_inc(
                    wqk_loaded[1], 16
                )
                sp.dma_start(w_p[:].bitcast(F32), p_hl[0]).then_inc(wp_loaded, 16)
                twins(0)
                load_wqk(2, ("qk", 0))
                wait_filled(("v", ST - 1))
                sp.dma_start(w_v[:].bitcast(F32), v1_hl.rearrange("p a (k n) -> p a k n", k=KT)).then_inc(wv_loaded, 16)
                twins(1)
                load_wqk(3, ("qk", 1))

                def spread_denominators(h):
                    sp.wait_ge(drained["acc"], use(b, ("pv", h), done=1))
                    row = rows_of(h + 1).start
                    sp.dma_start(den_c[:], hf[row : row + 1, :]).then_inc(den_spread, 16)

                def return_inverses(h):
                    sp.wait_ge(rden_ready, b * (HEADS - 1) + h + 1)
                    sp.dma_start(rden_row[h % 2].rearrange("(p c) -> p c", p=P), rden_c[:]).then_inc(rden_out, 16)
                    if h % 2 == 0 and h:
                        wait_filled(("proj", h // 2 - 1, KT - 1))
                        sp.dma_start(w_p[:].bitcast(F32), p_hl[h // 2]).then_inc(wp_loaded, 16)
                    sp.wait_ge(rden_out, 16 * (b * (HEADS - 1) + h + 1))
                    sp.dma_start(
                        hl[rows_of(h), :].bitcast(F32), rden_row[h % 2 : h % 2 + 1, :].to_broadcast([D, N])
                    ).then_inc(rden_back, 16)

                for h in range(1, HEADS):
                    spread_denominators(h - 1)
                    if h + 1 < HEADS:
                        twins(h + 1)
                    if h + 3 < HEADS:
                        load_wqk(h + 3, ("qk", h + 1))
                    if h == HEADS - 2:
                        load_wqk(0, ("qk", HEADS - 2))
                        load_wqk(HEADS, ("qk", HEADS - 1))
                    return_inverses(h - 1)
                    if h == PROJ_HEADS[0]:
                        what = ("proj", 0, KT - 1)
                        sp.wait_ge(drained[pair_of(what)], use(b, what, done=1))
                        sp.dma_start(x_in[:], x[bass.ds(following, 1)].rearrange("b p k n -> (b p) k n")).then_inc(
                            x_loaded, 16
                        )
                wait_filled(("v1", ST - 1))
                sp.dma_start(w_v[:].bitcast(F32), v_hl.rearrange("p a (k n) -> p a k n", k=KT)).then_inc(wv_loaded, 16)
                for n in range(NH):
                    sp.wait_ge(out_ready, 1 + b * NH + n + 1)
                    sp.dma_start(
                        out[bass.ds(b, 1)].rearrange("b p k n -> (b p) k n")[:, :, half(n)], x_mid[:, :, half(n)]
                    ).then_inc(out_done, 16)
            sp.wait_ge(x_loaded, (B + 1) * 16)
            sp.wait_ge(wqk_loaded[0], (B * HEADS // 2 + 1) * 16)
            sp.wait_ge(wv_loaded, (2 * B + 1) * 16)
            sp.wait_ge(out_done, 16 + B * NH * 16)

        @block.gpsimd
        def _(pool):
            pool.sem_inc(h_lo, 1)
            nc.gpsimd.memset(minus_half, -0.5)
            nc.gpsimd.memset(ones[:].bitcast(F32), 1.0)
            nc.gpsimd.memset(k_h1[0][:].bitcast(F32), 1.0)
            nc.gpsimd.memset(k_h1[1][:].bitcast(F32), 1.0).then_inc(ones_set, 1)
            pool.wait_ge(ones_set, 1)
            pool.wait_ge(drained["s1"], use(None, ("var",), done=1))
            nc.gpsimd.tensor_tensor(rstd_c, var_c, minus_half, ALU.pow).then_inc(rstd_ready, 1)
            with pool.Fori(0, B) as b:
                pool.wait_ge(pv_done, 1 + b * TILES)
                nc.gpsimd.tensor_tensor(unused, minus_half, minus_half, ALU.add)
                for j in range(ST):
                    nc.gpsimd.memset(vh[:, j, :, 1, :].bitcast(F32), 1.0)
                    last = nc.gpsimd.memset(vl[:, j, :, 1, :].bitcast(F32), 0.0)
                last.then_inc(ones_set, 1)
                for h in range(HEADS):
                    pool.wait_ge(h_hi, b * HEADS + h + 1)
                    r, c = rows_of(h), slice(0, HALF if h == HEADS - 1 else N)
                    nc.gpsimd.tensor_tensor(hl[r, c], hf[r, c], hh[r, c].bitcast(F32), ALU.subtract).then_inc(h_lo, 1)
                    pool.wait_ge(h_lo, 1 + b * HEADS + h + 1)
                pool.wait_ge(drained["s1"], use(b, ("var",), done=1))
                nc.gpsimd.tensor_tensor(rstd_c, var_c, minus_half, ALU.pow).then_inc(rstd_ready, 1)

        @block.scalar
        def _(act):
            act.sem_inc(t1_drained, 1)
            for r in range(3):
                act.wait_ge(w_in, 16 * (1, 3, 5)[r])
                if r:
                    act.wait_ge(w_out, 16 * (0, 2, 6)[r])
                cut = (slice(0, 4), slice(0, 4), slice(0, 2))[r]
                last = nc.scalar.activation(xh[:, cut, :], x_in[:, cut, :], ACT.Copy)
                if r == 2:
                    last = nc.scalar.activation(xh[:, 2, 0 : KT * P], x_in[:, 2, 0 : KT * P], ACT.Copy)
                last.then_inc(w_hi, 1)
            act.wait_ge(consts_in, 16 * 8)
            act.wait_ge(w_out, 10 * 16)

            def norm_hi_part(image, k):
                act.wait_ge(y_ready, image * KT + k + 1)
                nc.scalar.activation(xh[:, k, :], y_of[k], ACT.Identity, bias=nb_c[:, k : k + 1]).then_inc(norm_hi, 1)

            for k in range(KT):
                norm_hi_part(0, k)

            with act.Fori(0, B) as b:

                def wait_filled(what, pair=None):
                    act.wait_ge(filled[pair or pair_of(what)], filling(b, what, pair))

                def exps(i, pair_drained, src, width, scale):
                    w = slice(0, width)
                    act.wait_ge(hi_done, 1 + b * TILES + max(i - 1, 0))
                    nc.scalar.activation(eh[i % 2][:, w], src, ACT.Exp, scale=scale).then_inc(e_hi, 1)
                    act.wait_ge(e_lo, 1 + b * TILES + i)
                    nc.scalar.activation(ef[:, w], src, ACT.Exp, scale=scale).then_inc(pair_drained, 1)

                def split_qk(h):
                    wait_filled(("qk", h))
                    nc.scalar.activation(q_hh[h % 2][0:D, :], bank["misc"][0:D, :], ACT.Copy)
                    nc.scalar.activation(k_h1[h % 2][0:D, :], bank["misc"][D:P, :], ACT.Copy).then_inc(qk_hi, 1)

                def max_row(h):
                    wait_filled(("row", h))
                    nc.scalar.activation(q_lm[slot_of(h)][D : D + 1, :], bank["s0"][0:1, :], ACT.Copy, scale=-1.0).then_inc(
                        drained["s0"], 1
                    )

                def copy_head(h):
                    act.wait_ge(pv_done, 1 + b * TILES + (h + 1) * ST)
                    act.wait_ge(h_lo, 1 + b * HEADS + h)
                    if h == 0:
                        act.wait_ge(out_ready, 1 + b * NH)
                    nc.scalar.activation(hf[:], bank["acc"][:], ACT.Copy).then_inc(drained["acc"], 1)

                def head_hi(h):
                    act.wait_ge(h_scaled, b * HEADS + h + 1)
                    r = rows_of(h)
                    nc.scalar.activation(hh[r, :], hf[r, :], ACT.Copy).then_inc(h_hi, 1)

                split_qk(0)
                for j in range(ST):
                    wait_filled(("v", j))
                    nc.scalar.activation(
                        vh[:, j, :, 0:3:2, :],
                        bank[S[j % 2]][:, 0:C].rearrange("p (a c d) -> p a c d", c=2, d=D),
                        ACT.Copy,
                    ).then_inc(v_hi, 1)
                max_row(0)
                split_qk(1)
                for h in range(HEADS):
                    for j in range(ST):
                        wait_filled(("s", h, j))
                        exps(h * ST + j, drained[S[j % 2]], bank[S[j % 2]][:], N, SCALE)
                        if j == 0 and 1 <= h < HEADS - 1:
                            split_qk(h + 1)
                        if h and j == SCALE_AT[(h - 1) % 2] + 1:
                            head_hi(h - 1)
                    if h + 1 < HEADS:
                        max_row(h + 1)
                        copy_head(h)
                r = rows_of(HEADS - 1)
                for n in range(NH):
                    if n == 0:
                        act.wait_ge(h_scaled, (b + 1) * HEADS)
                    else:
                        act.wait_ge(drained["acc"], use(b, ("pv", HEADS - 1), done=1))
                    nc.scalar.activation(hh[r, half(n)], hf[r, half(n)], ACT.Copy).then_inc((h_hi, tail_hi)[n], 1)

                for n in range(NH):
                    for m in range(KT):
                        what = ("proj", LAST, m, n)
                        act.wait_ge(drained[pair_of(what)], use(b, what, done=1))
                        nc.scalar.activation(xh[:, m, half(n)], x_mid[:, m, half(n)], ACT.Copy).then_inc(mid_hi, 1)

                def split_g(n):
                    wait_filled(("g", n))
                    for dst, r in ((q_hh[1], slice(0, P)), (k_h1[1], slice(0, D)), (k_hl[1], slice(0, D))):
                        last = nc.scalar.activation(
                            dst[r, half(n)], bank["misc"][r, half(n)], ACT.Identity, bias=bq_c[r, :]
                        )
                    last.then_inc(g_hi, 1)

                split_g(0)
                for j in range(ST):
                    if j == 2:
                        split_g(1)
                    wait_filled(("v1", j))
                    nc.scalar.activation(
                        vh[:, j].rearrange("p a c d -> p (a c d)")[:, 0:C], bank[S[j % 2]][:, 0:C], ACT.Copy
                    ).then_inc(v_hi, 1)
                max_row(HEADS)

                def copy_outputs(n):
                    if n == 0:
                        act.wait_ge(norm_lo, (b + 2) * KT)
                    else:
                        act.wait_ge(out_ready, 1 + b * NH + n)
                    wait_filled(("den", n))
                    nc.scalar.activation(hf[:, half(0)], bank["s1"][:, half(0)], ACT.Copy).then_inc(drained["s1"], 1)
                    wait_filled(("o", n), "acc")
                    nc.scalar.activation(hh_f[:], bank["acc"][:], ACT.Copy).then_inc(drained["acc"], 1)

                for i in range(NH * ST):
                    act.wait_ge(t1_filled, b * NH * ST + i + 1)
                    exps(HEADS * ST + i, t1_drained, bank["s0"][:, half(i % 2)], HALF, 1.0)
                    if i < ST:
                        for k in NORM_HI.get(i, ()):
                            norm_hi_part(b + 1, k)
                    if i == ST:
                        copy_outputs(0)
                copy_outputs(1)

        @block.vector
        def _(dve):
            dve.sem_inc(e_lo, 1)
            dve.sem_inc(out_ready, 1)
            for n in drained:
                dve.sem_inc(drained[n], 1)
            for r in range(3):
                dve.wait_ge(w_hi, r + 1)
                if r:
                    dve.wait_ge(w_out, 16 * (0, 2, 6)[r])
                cut = (slice(0, 4), slice(0, 4), slice(0, 2))[r]
                last = nc.vector.tensor_tensor(
                    xl[:, cut, :], x_in[:, cut, :], xh[:, cut, :].bitcast(F32), ALU.subtract
                )
                if r == 2:
                    w = slice(0, KT * P)
                    last = nc.vector.tensor_tensor(xl[:, 2, w], x_in[:, 2, w], xh[:, 2, w].bitcast(F32), ALU.subtract)
                last.then_inc(w_split, 1)
            dve.wait_ge(consts_in, 16 * 8)
            first_links = [0]

            def first_link(ins):
                ins.then_inc(dve_step, 1)
                first_links[0] += 1
                dve.wait_ge(dve_step, first_links[0])

            first_link(nc.vector.tensor_scalar(gb_c, bv_c, gamma_c, None, ALU.mult))
            dve.wait_ge(w_out, 10 * 16)

            def statistics(k, n):
                return nc.vector.bn_stats(stats[:, k, n, :], x_in[:, k, half(n)])

            def channel_moments(link, last_stats):
                link(last_stats)
                nc.vector.memset(dev_c, 0.0)
                for k in range(KT):
                    last = nc.vector.bn_aggr(mv[:, k, :], stats[:, k, :, :])
                last.then_inc(stat_ready, 1)

            def group_mean(b, image, link):
                dve.wait_ge(stat_ready, image * 2 + 1)
                dve.wait_ge(filled["s1"], filling(b, ("mean",)))
                nc.vector.tensor_copy(mean_c, bank["s1"][:, HALF : HALF + KT]).then_inc(drained["s1"], 1)
                dve.wait_ge(drained["s1"], use(b, ("mean",), done=1))
                link(nc.vector.tensor_tensor(dev_c, mv[:, :, 0], mean_c, ALU.subtract))
                link(nc.vector.tensor_tensor(dev_c, dev_c, dev_c, ALU.mult))
                nc.vector.tensor_tensor(dev_c, dev_c, mv[:, :, 1], ALU.add).then_inc(stat_ready, 1)

            def group_variance(b, image, link):
                dve.wait_ge(filled["s1"], filling(b, ("var",)))
                nc.vector.tensor_scalar(var_c, bank["s1"][:, HALF : HALF + KT], EPS, None, ALU.add).then_inc(
                    drained["s1"], 1
                )
                dve.wait_ge(rstd_ready, image + 1)
                link(nc.vector.tensor_tensor(fac_c, rstd_c, nw_c, ALU.mult))

            def norm_y(k):
                c = slice(k, k + 1)
                nc.vector.tensor_scalar(
                    y_of[k], x_in[:, k, :], mean_c[:, c], fac_c[:, c], ALU.subtract, ALU.mult
                ).then_inc(y_ready, 1)

            def norm_lo_part(image, k):
                dve.wait_ge(norm_hi, image * KT + k + 1)
                nc.vector.scalar_tensor_tensor(
                    out=xl[:, k, :], in0=y_of[k], scalar=nb_c[:, k : k + 1],
                    in1=xh[:, k, :].bitcast(F32), op0=ALU.add, op1=ALU.subtract,
                ).then_inc(norm_lo, 1)

            dve.wait_ge(x_loaded, 16)
            for k, n in STATS_AT.values():
                last = statistics(k, n)
            channel_moments(first_link, last)
            group_mean(None, 0, first_link)
            group_variance(None, 0, first_link)
            for k in range(KT):
                norm_y(k)
            for k in range(KT):
                norm_lo_part(0, k)
            assert first_links[0] == START_LINKS, first_links

            with dve.Fori(0, B) as b:
                steps = [0]

                def link(ins):
                    ins.then_inc(dve_step, 1)
                    steps[0] += 1
                    dve.wait_ge(dve_step, b * DVE_LINKS + START_LINKS + steps[0])

                def wait_filled(what, pair=None):
                    dve.wait_ge(filled[pair or pair_of(what)], filling(b, what, pair))

                def drain(ins, what, pair=None):
                    ins.then_inc(drained[pair or pair_of(what)], 1)

                def exp_lo(i, pair_drained, done, width):
                    w = slice(0, width)
                    dve.wait_ge(pair_drained, done)
                    dve.wait_ge(pv_done, 1 + b * TILES + max(i - 1, 0))
                    nc.vector.tensor_tensor(
                        el[i % 2][:, w], ef[:, w], eh[i % 2][:, w].bitcast(F32), ALU.subtract
                    ).then_inc(e_lo, 1)

                def row_max(h, t):
                    what = ("max", h, t)
                    wait_filled(what)
                    drain(nc.vector.reduce_max(mx[slot_of(h)][:, t : t + 1], bank[pair_of(what)][:], AX_X), what)

                def add_proj(p, m):
                    what = ("proj", p, m)
                    wait_filled(what)
                    if p == 0 and m == 0:
                        dve.wait_ge(out_done, 16 + b * NH * 16)
                    ps = bank[pair_of(what)]
                    if p == 0:
                        ins = nc.vector.scalar_tensor_tensor(
                            out=x_mid[:, m, :], in0=ps[:], scalar=pb_c[:, m : m + 1], in1=x_in[:, m, :],
                            op0=ALU.add, op1=ALU.add,
                        )
                    else:
                        ins = nc.vector.tensor_tensor(x_mid[:, m, :], ps[:], x_mid[:, m, :], ALU.add)
                    drain(ins, what)

                def lo_qk(h):
                    ps = bank["misc"]
                    dve.wait_ge(qk_hi, b * HEADS + h + 1)
                    s = h % 2
                    nc.vector.tensor_tensor(q_lm[s][0:D, :], ps[0:D, :], q_hh[s][0:D, :].bitcast(F32), ALU.subtract)
                    drain(
                        nc.vector.tensor_tensor(k_hl[s][D:P, :], ps[D:P, :], k_h1[s][0:D, :].bitcast(F32), ALU.subtract),
                        ("qk", h),
                    )

                def invert_denominators(h):
                    dve.wait_ge(den_spread, 16 * (b * (HEADS - 1) + h + 1))
                    nc.vector.reciprocal(rden_c[:], den_c[:]).then_inc(rden_ready, 1)

                def scale_head(h):
                    dve.wait_ge(rden_back, 16 * (b * (HEADS - 1) + h + 1))
                    r = rows_of(h)
                    nc.vector.tensor_tensor(hf[r, :], hf[r, :], hl[r, :].bitcast(F32), ALU.mult).then_inc(h_scaled, 1)

                lo_qk(0)
                for j in range(ST):
                    dve.wait_ge(v_hi, b * 2 * ST + j + 1)
                    drain(
                        nc.vector.tensor_tensor(
                            vl[:, j, :, 0:3:2, :],
                            bank[S[j % 2]][:, 0:C].rearrange("p (a c d) -> p a c d", c=2, d=D),
                            vh[:, j, :, 0:3:2, :].bitcast(F32),
                            ALU.subtract,
                        ),
                        ("v", j),
                    )
                    for t in MAX_WITH_V.get(j, ()):
                        row_max(0, t)
                lo_qk(1)
                for h in range(HEADS):
                    for j in range(ST):
                        exp_lo(h * ST + j, drained[S[j % 2]], use(b, ("s", h, j), done=1), N)
                        if j == 0 and 1 <= h < HEADS - 1:
                            lo_qk(h + 1)
                        if h and j == 2:
                            invert_denominators(h - 1)
                        if h and j == SCALE_AT[(h - 1) % 2]:
                            scale_head(h - 1)
                        if h + 1 < HEADS and j in MAX_BETWEEN:
                            row_max(h + 1, MAX_BETWEEN[j])
                        if h in PROJ_HEADS and j in PROJ_BETWEEN:
                            add_proj(h // 2 - 1, PROJ_BETWEEN[j])
                        if h + 1 < HEADS and j in MAX_AFTER:
                            row_max(h + 1, MAX_AFTER[j])
                        if h == HEADS - 1:
                            if j == 0:
                                dve.wait_ge(x_loaded, (b + 2) * 16)
                            last = statistics(*STATS_AT[j])
                channel_moments(link, last)

                dve.wait_ge(pv_done, 1 + b * TILES + HEADS * ST)
                r, den_rows = rows_of(HEADS - 1), rows_of(HEADS)
                for n in range(NH):
                    link(nc.vector.reciprocal(hf[r, half(n)], bank["acc"][den_rows, half(n)]))
                    nc.vector.tensor_tensor(hf[r, half(n)], bank["acc"][r, half(n)], hf[r, half(n)], ALU.mult).then_inc(
                        (h_scaled, drained["acc"])[n], 1
                    )
                dve.wait_ge(tail_hi, b + 1)
                nc.vector.tensor_tensor(
                    hl[r, half(1)], hf[r, half(1)], hh[r, half(1)].bitcast(F32), ALU.subtract
                ).then_inc(tail_lo, 1)

                for n in range(NH):
                    for m in range(KT):
                        what = ("proj", LAST, m, n)
                        wait_filled(what)
                        x_part = x_mid[:, m, half(n)]
                        drain(nc.vector.tensor_tensor(x_part, bank[pair_of(what)][:, half(n)], x_part, ALU.add), what)
                    for m in range(KT):
                        dve.wait_ge(mid_hi, b * NH * KT + n * KT + m + 1)
                        nc.vector.tensor_tensor(
                            xl[:, m, half(n)], x_mid[:, m, half(n)], xh[:, m, half(n)].bitcast(F32), ALU.subtract
                        ).then_inc(mid_lo, 1)

                def lo_g(n):
                    dve.wait_ge(g_hi, b * NH + n + 1)
                    for dst, r in ((q_lm[1], slice(0, D)), (k_hl[1], slice(D, P))):
                        last = nc.vector.scalar_tensor_tensor(
                            out=dst[r, half(n)], in0=bank["misc"][r, half(n)], scalar=bq_c[r, :],
                            in1=q_hh[1][r, half(n)].bitcast(F32), op0=ALU.add, op1=ALU.subtract,
                        )
                    drain(last, ("g", n))

                lo_g(0)
                for j in range(ST):
                    if j == 2:
                        lo_g(1)
                    dve.wait_ge(v_hi, b * 2 * ST + ST + j + 1)
                    v_of = [t[:, j].rearrange("p a c d -> p (a c d)")[:, 0:C] for t in (vl, vh)]
                    drain(
                        nc.vector.tensor_tensor(v_of[0], bank[S[j % 2]][:, 0:C], v_of[1].bitcast(F32), ALU.subtract),
                        ("v1", j),
                    )
                    for t in MAX_WITH_V.get(j, ()):
                        row_max(HEADS, t)
                def copy_outputs(n):
                    if n == 0:
                        dve.wait_ge(norm_lo, (b + 2) * KT)
                    dve.wait_ge(pv_done, 1 + b * TILES + (HEADS + n + 1) * ST)
                    drain(nc.vector.tensor_copy(hl_f[:], bank["misc"][:]), ("o", n), "misc")
                    dve.wait_ge(drained["s1"], use(b, ("den", n), done=1))
                    link(nc.vector.reciprocal(hf[:, half(1)], hf[:, half(0)]))

                def output(n, m):
                    if m == 0:
                        link(nc.vector.tensor_scalar(hf[:, half(1)], hf[:, half(1)], gamma_c, None, ALU.mult))
                        dve.wait_ge(drained["acc"], use(b, ("o", n), "acc", done=1))
                    if m == KT // 2:
                        dve.wait_ge(drained["misc"], use(b, ("o", n), "misc", done=1))
                    return nc.vector.tensor_tensor(outs[m], outs[m], hf[:, half(1)], ALU.mult)

                def add_output(n, m):
                    last = nc.vector.scalar_tensor_tensor(
                        out=x_mid[:, m, half(n)], in0=outs[m], scalar=gb_c[:, m : m + 1],
                        in1=x_mid[:, m, half(n)], op0=ALU.add, op1=ALU.add,
                    )
                    if m == KT - 1:
                        last.then_inc(out_ready, 1)

                for n in range(NH):
                    for j in range(ST):
                        i = n * ST + j
                        exp_lo(HEADS * ST + i, t1_drained, 1 + b * NH * ST + i + 1, HALF)
                        if n == 0:
                            if j == MEAN_AT + 1:
                                group_mean(b, b + 1, link)
                            if j == VAR_AT + 1:
                                group_variance(b, b + 1, link)
                            for k in NORM_Y.get(j, ()):
                                if j == min(NORM_Y) and k == 0:
                                    dve.wait_ge(h_lo, 1 + (b + 1) * HEADS)
                                norm_y(k)
                            for k in NORM_LO.get(j, ()):
                                norm_lo_part(b + 1, k)
                        else:
                            if j == 0:
                                copy_outputs(0)
                            for m in OUTPUT_AT.get(j, ()):
                                link(output(0, m))
                                add_output(0, m)
                dve.wait_ge(out_ready, 1 + b * NH + 1)
                copy_outputs(1)
                for m in range(KT):
                    link(output(1, m))
                    add_output(1, m)
                dve.wait_ge(out_ready, 1 + (b + 1) * NH)
                assert steps[0] == DVE_LINKS, steps

        @block.tensor
        def _(pe):
            pe.sem_inc(hi_done, 1)
            pe.sem_inc(pv_done, 1)
            pe.wait_ge(consts_in, 16 * 8)
            pe.wait_ge(ones_set, 1)

            def group_average(b, what, image, values):
                pe.wait_ge(stat_ready, image * 2 + (1 if what == ("mean",) else 2))
                pe.wait_ge(drained["s1"], use(b, what))
                nc.tensor.matmul(bank["s1"][:, HALF : HALF + KT], grp[:], values, start=True, stop=True).then_inc(
                    filled["s1"], 1
                )

            group_average(None, ("mean",), 0, mv[:, :, 0])
            group_average(None, ("var",), 0, dev_c)

            with pe.Fori(0, B) as b:

                def wait_free(what, pair=None):
                    pe.wait_ge(drained[pair or pair_of(what)], use(b, what, pair))

                def fill(ins, what, pair=None):
                    ins.then_inc(filled[pair or pair_of(what)], 1)

                def product(ps, hi_lo_pairs):
                    n = len(hi_lo_pairs)
                    for k, ((wh_, wl_), (mh, ml)) in enumerate(hi_lo_pairs):
                        nc.tensor.matmul(ps, wh_, mh, start=k == 0, stop=False)
                        nc.tensor.matmul(ps, wh_, ml, start=False, stop=False)
                        last = nc.tensor.matmul(ps, wl_, mh, start=False, stop=k == n - 1)
                    return last

                def project_v(j, what):
                    if what in (("v1", 0), ("v1", 1)):
                        pair = pair_of(what)
                        pe.wait_ge(drained[pair], use(b, ("proj", LAST, 1 + j, 1)))
                    else:
                        wait_free(what)
                    t = slice(j * P, (j + 1) * P)
                    fill(
                        product(
                            bank[pair_of(what)][:, 0:C],
                            [((xh[:, k, t], xl[:, k, t]), (w_v[:, 0, k, :], w_v[:, 1, k, :])) for k in range(KT)],
                        ),
                        what,
                    )

                def project_qk(w, what, n):
                    last = product(
                        bank[pair_of(what)][:, half(n)],
                        [((w[:, 0, k, :], w[:, 1, k, :]), (xh[:, k, half(n)], xl[:, k, half(n)])) for k in range(KT)],
                    )
                    if n == NH - 1:
                        fill(last, what)

                def qk_half(h, n):
                    if n == 0:
                        wait_free(("qk", h))
                        loads = HEADS // 2 + h % 2
                        pe.wait_ge(wqk_loaded[h % 2], 16 * (b * loads + h // 2 + 1))
                    project_qk(w_qk[h % 2], ("qk", h), n)

                def max_tile(h, t):
                    what = ("max", h, t)
                    wait_free(what)
                    for n in range(NH):
                        last = nc.tensor.matmul(
                            bank[pair_of(what)][:, half(n)], q_hh[slot_of(h)][0:D, t * P : (t + 1) * P],
                            k_h1[slot_of(h)][0:D, half(n)], start=True, stop=True,
                        )
                    fill(last, what)

                def max_row(h):
                    for p in ("misc", "acc") if h in (0, HEADS) else ("misc",):
                        t = max(t for t in range(ST) if ("max", h, t) in USES[p])
                        pe.wait_ge(drained[p], use(b, ("max", h, t), done=1))
                    wait_free(("row", h))
                    for t in range(ST):
                        last = nc.tensor.transpose(
                            bank["s0"][0:1, t * P : (t + 1) * P], mx[slot_of(h)][:, t : t + 1], eye[:]
                        )
                    fill(last, ("row", h))

                def scores(s, ps, j, n):
                    keys = slice(j * P, (j + 1) * P)
                    nc.tensor.matmul(ps, k_hl[s][:, keys], q_hh[s][:, half(n)], start=True, stop=False)
                    return nc.tensor.matmul(
                        ps, k_h1[s][0 : D + 1, keys], q_lm[s][0 : D + 1, half(n)], start=False, stop=True
                    )

                def head_scores(h, j):
                    what = ("s", h, j)
                    wait_free(what)
                    if j == 0:
                        pe.wait_ge(qk_twin[h % 2], 32 * (b * (HEADS // 2) + h // 2 + 1))
                        pe.wait_ge(drained["misc"], use(b, ("qk", h), done=1))
                    for n in range(NH):
                        last = scores(h % 2, bank[S[j % 2]][:, half(n)], j, n)
                    fill(last, what)

                def head_pv_hi(h, j):
                    i = h * ST + j
                    if j == 0:
                        wait_free(("pv", h))
                    pe.wait_ge(e_hi, b * TILES + i + 1)
                    for n in range(NH):
                        ps, moving = bank["acc"][:, half(n)], eh[i % 2][:, half(n)]
                        nc.tensor.matmul(ps, head_v(vh, h, j), moving, start=j == 0, stop=False)
                        last = nc.tensor.matmul(ps, head_v(vl, h, j), moving, start=False, stop=False)
                    last.then_inc(hi_done, 1)

                def head_pv_lo(h, j):
                    i = h * ST + j
                    pe.wait_ge(e_lo, 1 + b * TILES + i + 1)
                    for n in range(NH):
                        last = nc.tensor.matmul(
                            bank["acc"][:, half(n)], head_v(vh, h, j), el[i % 2][:, half(n)],
                            start=False, stop=j == ST - 1,
                        )
                    last.then_inc(pv_done, 1)

                def project_out(p, m):
                    what = ("proj", p, m)
                    wait_free(what)
                    if m == 0:
                        pe.wait_ge(wp_loaded, 16 * (b * KT + p + 1))
                        pe.wait_ge(h_lo, 1 + b * HEADS + 2 * p + 2)
                    c = slice(m * P, (m + 1) * P)
                    for n in range(NH):
                        last = product(
                            bank[pair_of(what)][:, half(n)],
                            [((w_p[:, 0, c], w_p[:, 1, c]), (hh[:, half(n)], hl[:, half(n)]))],
                        )
                    fill(last, what)

                pe.wait_ge(norm_lo, (b + 1) * KT)
                for n in range(NH):
                    qk_half(0, n)
                pe.wait_ge(wv_loaded, 16 * (2 * b + 1))
                pe.wait_ge(t1_drained, 1 + b * NH * ST)
                for j in range(ST):
                    project_v(j, ("v", j))
                    for t in MAX_WITH_V.get(j, ()):
                        if t == 0:
                            pe.wait_ge(drained["misc"], use(b, ("qk", 0), done=1))
                        max_tile(0, t)
                max_row(0)
                for n in range(NH):
                    qk_half(1, n)
                pe.wait_ge(ones_set, b + 2)
                head_scores(0, 0)
                for h in range(HEADS):
                    for j in range(ST):
                        if j + 1 < ST:
                            head_scores(h, j + 1)
                        if h + 1 < HEADS and j in MAX_BETWEEN:
                            max_tile(h + 1, MAX_BETWEEN[j])
                        if h in PROJ_HEADS and j in PROJ_BETWEEN:
                            project_out(h // 2 - 1, PROJ_BETWEEN[j])
                        head_pv_hi(h, j)
                        if j:
                            head_pv_lo(h, j - 1)
                        if h + 1 < HEADS and j in MAX_AFTER:
                            max_tile(h + 1, MAX_AFTER[j])
                    if h + 1 < HEADS:
                        max_row(h + 1)
                    if h + 2 < HEADS:
                        qk_half(h + 2, 0)
                    head_pv_lo(h, ST - 1)
                    if h + 1 < HEADS:
                        head_scores(h + 1, 0)
                    if h + 2 < HEADS:
                        qk_half(h + 2, 1)

                pe.wait_ge(wp_loaded, 16 * (b + 1) * KT)
                for n in range(NH):
                    if n == 0:
                        pe.wait_ge(h_lo, 1 + (b + 1) * HEADS)
                    else:
                        pe.wait_ge(tail_lo, b + 1)
                    for m in range(KT):
                        what = ("proj", LAST, m, n)
                        if n == 0:
                            wait_free(what)
                        c = slice(m * P, (m + 1) * P)
                        fill(
                            product(
                                bank[pair_of(what)][:, half(n)],
                                [((w_p[:, 0, c], w_p[:, 1, c]), (hh[:, half(n)], hl[:, half(n)]))],
                            ),
                            what,
                        )

                def project_g(n):
                    if n == 0:
                        pe.wait_ge(wqk_loaded[1], 16 * (b + 1) * (HEADS // 2 + 1))
                    pe.wait_ge(drained["misc"], use(b, ("proj", LAST, 0, n), done=1))
                    w = w_qk[1]
                    for k in range(KT):
                        pe.wait_ge(mid_lo, b * NH * KT + n * KT + k + 1)
                        for i, (stat, moving) in enumerate(((0, xh), (0, xl), (1, xh))):
                            last = nc.tensor.matmul(
                                bank["misc"][:, half(n)], w[:, stat, k, :], moving[:, k, half(n)],
                                start=k == 0 and i == 0, stop=k == KT - 1 and i == 2,
                            )
                    fill(last, ("g", n))

                project_g(0)
                pe.wait_ge(wv_loaded, 16 * (2 * b + 2))
                for j in range(ST):
                    if j == 2:
                        project_g(1)
                    project_v(j, ("v1", j))
                    for t in MAX_WITH_V.get(j, ()):
                        if t == 0:
                            pe.wait_ge(drained["misc"], use(b, ("g", 1), done=1))
                        max_tile(HEADS, t)
                max_row(HEADS)

                def scores1(i):
                    n, j = divmod(i, ST)
                    if i == 0:
                        pe.wait_ge(drained["s0"], use(b, ("row", HEADS), done=1))
                    pe.wait_ge(t1_drained, 1 + b * NH * ST + max(i - 1, 0))
                    scores(1, bank["s0"][:, half(i % 2)], j, n).then_inc(t1_filled, 1)

                den = bank["s1"][:, half(0)]

                def out_of(m):
                    return bank[("acc", "misc")[m // 2]][:, half(m % 2)]

                def v1_of(tile, j, m):
                    return tile[:, j].rearrange("p a c d -> p (a c d)")[:, m * P : (m + 1) * P]

                def pv_hi1(n, j):
                    i = HEADS * ST + n * ST + j
                    if j == 0:
                        wait_free(("o", n), "acc")
                        wait_free(("o", n), "misc")
                        wait_free(("mean",) if n == 0 else ("den", n))
                    pe.wait_ge(e_hi, b * TILES + i + 1)
                    moving = eh[i % 2][:, 0:HALF]
                    nc.tensor.matmul(den, ones[:], moving, start=j == 0, stop=False)
                    for m in range(KT):
                        nc.tensor.matmul(out_of(m), v1_of(vh, j, m), moving, start=j == 0, stop=False)
                        last = nc.tensor.matmul(out_of(m), v1_of(vl, j, m), moving, start=False, stop=False)
                    last.then_inc(hi_done, 1)

                def pv_lo1(n, j):
                    i = HEADS * ST + n * ST + j
                    end = j == ST - 1
                    pe.wait_ge(e_lo, 1 + b * TILES + i + 1)
                    moving = el[i % 2][:, 0:HALF]
                    last = nc.tensor.matmul(den, ones[:], moving, start=False, stop=end)
                    if end:
                        fill(last, ("den", n))
                    for m in range(KT):
                        last = nc.tensor.matmul(out_of(m), v1_of(vh, j, m), moving, start=False, stop=end)
                        if end and m == 1:
                            fill(last, ("o", n), "acc")
                    last.then_inc(pv_done, 1)

                scores1(0)
                for n in range(NH):
                    for j in range(ST):
                        if n * ST + j + 1 < NH * ST:
                            scores1(n * ST + j + 1)
                        pv_hi1(n, j)
                        if j:
                            pv_lo1(n, j - 1)
                        if n == 0 and j == MEAN_AT:
                            group_average(b, ("mean",), b + 1, mv[:, :, 0])
                        if n == 0 and j == VAR_AT:
                            group_average(b, ("var",), b + 1, dev_c)
                    pv_lo1(n, ST - 1)


def kernel(x, L0_conv_norm_w, L0_conv_norm_b, L0_conv_qkv_w, L0_conv_proj_w, L0_conv_proj_b, L1_conv_Wq, L1_conv_bq, L1_conv_Wv, L1_conv_bv, L1_conv_gamma):
    import concourse.bacc as bacc
    from concourse.bass_utils import run_bass_kernel_spmd

    def array(a):
        return np.ascontiguousarray(np.asarray(a))

    def by_channel(v):
        return array(v).reshape(KT, P).T

    def stationary(w):
        return array(w).reshape(-1, KT, P).transpose(2, 1, 0)

    qkv = array(L0_conv_qkv_w).reshape(HEADS, 3 * D, C)
    arrays = {
        "x": array(x).reshape(B, C, N),
        "wqk": qkv[:, 0 : 2 * D].reshape(HEADS, 2 * D, KT, P).transpose(3, 0, 2, 1).reshape(P, -1),
        "wv": stationary(qkv[:, 2 * D :].reshape(C, C)).reshape(P, -1),
        "wv1": stationary(L1_conv_Wv).reshape(P, -1),
        "wp": stationary(L0_conv_proj_w).reshape(P, -1),
        "wq1": stationary(np.concatenate([array(L1_conv_Wq)] * 2)).reshape(P, -1),
        "pb": by_channel(L0_conv_proj_b),
        "norm_w": by_channel(L0_conv_norm_w),
        "norm_b": by_channel(L0_conv_norm_b),
        "bv1": by_channel(L1_conv_bv),
        "bq1": np.concatenate([array(L1_conv_bq)] * 2).reshape(P, 1),
        "gamma": np.repeat(array(L1_conv_gamma), P).reshape(P, 1),
        "group": np.kron(np.eye(P * GROUPS // C), np.full((C // GROUPS,) * 2, GROUPS / C)).astype(np.float32),
        "ident": np.eye(P, dtype=np.float32),
    }
    nc = bacc.Bacc("TRN2", target_bir_lowering=False, num_devices=1)
    arrays = {f"in_{n}": array(a) for n, a in arrays.items()}
    aps = [nc.dram_tensor(n, a.shape, F32, kind="ExternalInput").ap() for n, a in arrays.items()]
    out = nc.dram_tensor("out", (B, C, N), F32, kind="ExternalOutput").ap()
    aps[0], out = (a.rearrange("b (k p) n -> b p k n", p=P) for a in (aps[0], out))
    attention_kernel(nc, *aps, out)
    result = run_bass_kernel_spmd(nc, [arrays], core_ids=[0])
    return result.results[0]["out"].reshape(np.shape(x))
```

```python
from contextlib import ExitStack

import numpy as np

import concourse.bass as bass
from concourse import mybir

B, C, N = 8, 512, 1024
P = 128
KT = C // P
ST = N // P
HEADS = 8
D = C // HEADS
HALF = 512
NH = N // HALF
GROUPS = 32
EPS = 1e-5
SCALE = float(D) ** -0.5

F32 = mybir.dt.float32
F32R = mybir.dt.float32r
ALU = mybir.AluOpType
ACT = mybir.ActivationFunctionType
AX_X = mybir.AxisListType.X

PROJ_BETWEEN = {1: 0, 2: 1, 3: 2, 4: 3}
PROJ_HEADS = (3, 5, 7)
INVERT_AT = 1
HEAD_HI_AT = {1: 6, 0: 7}
MAX_WITH_V = {2: (0, 1), 3: (2, 3), 4: (4, 5), 5: (6, 7)}
ROW_WITH_V = 6
STATS_AT = {0: (0,), 1: (1,), 2: (2,), 3: (3, 4), 5: (5, 6), 6: (7,)}
MEAN_AT, VAR_AT = 0, 1
NORM_Y = {3: (0, 1), 4: (2, 3)}
NORM_HI = {4: (0,), 5: (1, 2), 6: (3,)}
NORM_LO = {5: (0,), 6: (1, 2), 7: (3,)}
OUTPUT_AT = {2: (0,), 3: (1,), 4: (2,), 5: (3,)}
LAST = KT - 1
PIECES = (slice(0, HALF // 2), slice(HALF // 2, HALF), slice(HALF, N))
MISC = ("m0", "m1")


def extras(h, j):
    work = []
    if h in PROJ_HEADS and j in PROJ_BETWEEN and (h, j) != (HEADS - 1, min(PROJ_BETWEEN)):
        work.append(("proj", h // 2 - 1, PROJ_BETWEEN[j]))
    if h + 1 < HEADS:
        work.append(("max", h + 1, j))
    return work


def psum_uses():
    start = {"s0": [], "s1": [("mean",), ("var",)], "acc": [], "m0": [], "m1": []}
    s0, s1, acc, misc = [], [], [], ([], [])

    def both(*what):
        for n in range(NH):
            misc[n].append((*what, n))

    def max_tiles(h, tiles):
        for t in tiles:
            if t % 2:
                acc.append(("max", h, t))
            else:
                both("max", h, t)

    both("qk", 0)
    for j in range(ST):
        (s0, s1)[j % 2].append(("v", j))
        max_tiles(0, MAX_WITH_V.get(j, ()))
    acc.append(("row", 0))
    both("qk", 1)
    for h in range(HEADS):
        acc.append(("pv", h))
        for j in range(ST):
            (s0, s1)[j % 2].append(("s", h, j))
            for what in extras(h, j):
                both(*what)
        if h + 1 < HEADS:
            s0.append(("row", h + 1))
        if h + 2 < HEADS:
            both("qk", h + 2)
        if h == HEADS - 2:
            both("proj", LAST - 1, 0)
    both("proj", LAST, 0)
    for m, pair in ((1, s0), (2, s1), (3, acc)):
        for n in range(NH):
            pair.append(("proj", LAST, m, n))
    both("g")
    for j in range(ST):
        (s0, s1)[j % 2].append(("v1", j))
        max_tiles(HEADS, MAX_WITH_V.get(j, ()))
    acc.append(("row", HEADS))
    s1 += [("mean",), ("var",)]
    for n in range(NH):
        s1.append(("den", n))
        for pair in (acc, *misc):
            pair.append(("o", n))
    return start, {"s0": s0, "s1": s1, "acc": acc, "m0": misc[0], "m1": misc[1]}


START, USES = psum_uses()
TILES = HEADS * ST + NH * ST
START_LINKS = 5
DVE_LINKS = 7 + 6 * NH


def pair_of(what):
    return next(pair for pair in USES if what in USES[pair])


def slot_of(h):
    return 1 if h == HEADS else h % 2


def filling(b, what, pair=None):
    pair = pair or pair_of(what)
    if b is None:
        return START[pair].index(what) + 1
    signalled = [w for w in USES[pair] if not on_pv_done(w, pair)]
    return len(START[pair]) + b * len(signalled) + signalled.index(what) + 1


def on_pv_done(what, pair):
    return what[0] == "pv" or (what[0] == "o" and pair in MISC)


def use(b, what, pair=None, done=0):
    pair = pair or pair_of(what)
    if b is None:
        return 1 + START[pair].index(what) + done
    return 1 + len(START[pair]) + b * len(USES[pair]) + USES[pair].index(what) + done


def attention_kernel(nc, x, wqk, wv, wv1, wp, wq1, pb, norm_w, norm_b, bv1, bq1, gamma, group, ident, out):
    with ExitStack() as ctx:
        def sb(name, shape, dt=F32):
            return ctx.enter_context(nc.sbuf_tensor(name, shape, dt))

        def sem(name):
            return ctx.enter_context(nc.semaphore(name))

        qk_hl = nc.dram_tensor("qk_hl", [HEADS + 1, P, 2, KT * P], F32, kind="Internal").ap()
        v_hl = nc.dram_tensor("v_hl", [P, 2, KT * C], F32, kind="Internal").ap()
        v1_hl = nc.dram_tensor("v1_hl", [P, 2, KT * C], F32, kind="Internal").ap()
        p_hl = nc.dram_tensor("p_hl", [KT, P, 2, C], F32, kind="Internal").ap()

        rden_row = nc.dram_tensor("rden_row", [2, N], F32, kind="Internal").ap()

        v_shape = [P, ST, HEADS // 2, 3, D]
        with ExitStack() as shared:
            hh_f, hl_f, wp_f = (shared.enter_context(nc.sbuf_tensor(n, [P, N], F32)) for n in ("hh_f", "hl_f", "wp_f"))
            wv_f = shared.enter_context(nc.sbuf_tensor("wv_f", [P, 2, KT, C], F32))
            vl_f = shared.enter_context(nc.sbuf_tensor("vl_f", v_shape, F32))
        hh = sb("hh", [P, N], F32R)
        hl = sb("hl", [P, N], F32R)
        w_p = sb("w_p", [P, 2, C], F32R)
        w_v = sb("w_v", [P, 2, KT, C], F32R)
        vl = sb("vl", v_shape, F32R)
        vh = sb("vh", v_shape, F32R)
        x_in = sb("x_in", [P, KT, N])
        x_mid = sb("x_mid", [P, KT, N])
        xh = sb("xh", [P, KT, N], F32R)
        xl = sb("xl", [P, KT, N], F32R)
        w_qk = [sb(f"w_qk{i}", [P, 2, KT, P], F32R) for i in range(2)]
        k_hl = [sb(f"k_hl{i}", [P, N], F32R) for i in range(2)]
        q_hh = [sb(f"q_hh{i}", [P, N], F32R) for i in range(2)]
        k_h1 = [sb(f"k_h1{i}", [P, N], F32R) for i in range(2)]
        q_lm = [sb(f"q_lm{i}", [P, N], F32R) for i in range(2)]
        ef = sb("ef", [P, N])
        eh = [sb(f"eh{i}", [P, N], F32R) for i in range(2)]
        el = [sb(f"el{i}", [P, N], F32R) for i in range(2)]
        hf = sb("hf", [P, N])
        den_c, rden_c = sb("den_c", [P, N // P]), sb("rden_c", [P, N // P])
        ones = sb("ones", [P, P], F32R)
        eye = sb("eye", [P, P])
        grp = sb("grp", [P, P])
        row = sb("row", [ST, P], F32R)
        mx_half = sb("mx_half", [P, ST, NH])
        mx = [sb(f"mx{i}", [P, ST]) for i in range(2)]
        cols = sb("cols", [P, 5, KT])
        pb_c, nw_c, nb_c, bv_c, gb_c = (cols[:, i, :] for i in range(5))
        scal = sb("scal", [P, 2])
        bq_c, gamma_c = scal[:, 0:1], scal[:, 1:2]
        stats = sb("stats", [P, KT, NH, 6])
        mv = sb("mv", [P, KT, 2])
        gm = sb("gm", [P, 7, KT])
        mean_c, dev_c, var_c, rstd_c, fac_c, minus_half, unused = (gm[:, i, :] for i in range(7))

        bank = {n: ctx.enter_context(nc.psum_tensor(f"ps_{n}", [P, N], F32)) for n in ("s0", "s1", "acc", "misc")}
        S = ("s0", "s1")

        filled = {n: sem(f"{n}_filled") for n in USES}
        drained = {n: sem(f"{n}_drained") for n in USES}
        wqk_in, wv_in, w2_in = sem("wqk_in"), sem("wv_in"), sem("w2_in")
        w_hi, w_split, w2_hi, w2_split = sem("w_hi"), sem("w_split"), sem("w2_hi"), sem("w2_split")
        wqk_out, wv_out, w2_out = sem("wqk_out"), sem("wv_out"), sem("w2_out")
        consts_in, ones_set, x_loaded = sem("consts_in"), sem("ones_set"), sem("x_loaded")
        stat_ready, rstd_ready, y_ready = sem("stat_ready"), sem("rstd_ready"), sem("y_ready")
        norm_hi, norm_lo = sem("norm_hi"), sem("norm_lo")
        g_hi, tail_hi, tail_lo, max_ready = sem("g_hi"), sem("tail_hi"), sem("tail_lo"), sem("max_ready")
        row_back, tail_scaled, tail_end_lo = sem("row_back"), sem("tail_scaled"), sem("tail_end_lo")
        v_hi, mid_hi, mid_lo = sem("v_hi"), sem("mid_hi"), sem("mid_lo")
        wqk_loaded = [sem(f"wqk_loaded{i}") for i in range(2)]
        wv_loaded, wp_loaded = sem("wv_loaded"), sem("wp_loaded")
        qk_hi, qk_twin = sem("qk_hi"), [sem(f"qk_twin{i}") for i in range(2)]
        e_hi, e_lo, hi_done, pv_done = sem("e_hi"), sem("e_lo"), sem("hi_done"), sem("pv_done")
        h_hi, h_lo, h_scaled = sem("h_hi"), sem("h_lo"), sem("h_scaled")
        den_spread, rden_ready, rden_out, rden_back = (
            sem(n) for n in ("den_spread", "rden_ready", "rden_out", "rden_back")
        )
        t1_filled, t1_drained = sem("t1_filled"), sem("t1_drained")
        out_ready, out_done, dve_step = sem("out_ready"), sem("out_done"), sem("dve_step")

        def head_v(tile, h, j):
            start = (h // 2) * 3 * D + (h % 2) * D
            return tile[:, j].rearrange("p a c d -> p (a c d)")[:, start : start + P]

        def rows_of(h):
            return slice(D * (h % 2), D * (h % 2) + D)

        def half(n):
            return slice(n * HALF, (n + 1) * HALF)

        y_of = [hf[:], hh_f[:], hl_f[:], wp_f[:]]
        outs = [t[:, half(i)] for t in (hh_f, hl_f) for i in range(NH)]

        wqk_high, wqk_low, wqk_raw = (
            t[:].rearrange("p j a c d -> p (j a c d)")[:, 0 : HEADS * KT * P] for t in (vh, vl, vl_f)
        )
        wqk_parts = [wqk_high, wqk_low]
        w2_raw = [x_mid[:, i, :] for i in range(KT)]
        w2_high = [t[:] for t in (*eh, *el)]
        wq1_raw, wq1_high = ef[:, half(0)], ef[:, half(1)].bitcast(F32R)

        block = ctx.enter_context(nc.Block())

        @block.sync
        def _(sp):
            sp.sem_inc(out_done, 16)
            sp.sem_inc(row_back, 16)
            sp.sem_inc(wv_loaded, 16)
            sp.dma_start(wqk_raw, wqk).then_inc(wqk_in, 16)
            sp.dma_start(x_in[:], x[0]).then_inc(x_loaded, 16)
            for dst, src in (
                (cols[:, 0, :], pb), (cols[:, 1, :], norm_w), (cols[:, 2, :], norm_b), (cols[:, 3, :], bv1),
                (bq_c, bq1), (gamma_c, gamma), (eye[:], ident), (grp[:], group),
            ):
                sp.dma_start(dst, src).then_inc(consts_in, 16)
            sp.dma_start(wv_f[:, 1].rearrange("p k n -> p (k n)"), wv).then_inc(wv_in, 16)
            sp.dma_start(x_mid[:, 0:2, :].rearrange("p k n -> p (k n)"), wv1).then_inc(w2_in, 16)
            sp.dma_start(x_mid[:, 2:4, :].rearrange("p k n -> p (k n)"), wp).then_inc(w2_in, 16)
            sp.dma_start(wq1_raw, wq1).then_inc(w2_in, 16)
            sp.wait_ge(w_split, 1)
            for part in range(2):
                sp.dma_start(
                    w_qk[0][:, part].rearrange("p k n -> p (k n)").bitcast(F32), wqk_parts[part][:, 0 : KT * P].bitcast(F32)
                ).then_inc(wqk_loaded[0], 16)
            sp.wait_ge(w_split, KT)
            for part in range(2):
                sp.dma_start(
                    qk_hl[0:HEADS, :, part, :].rearrange("h p n -> p h n"),
                    wqk_parts[part].rearrange("p (h n) -> p h n", h=HEADS).bitcast(F32),
                ).then_inc(wqk_out, 16)
            for i in range(KT):
                sp.wait_ge(w2_split, i + 1)
                for part, tile in enumerate((w2_high[i].bitcast(F32), w2_raw[i])):
                    if i < KT // 2:
                        dst = v1_hl[:, part, i * N : (i + 1) * N]
                    else:
                        t = NH * (i - KT // 2)
                        dst = p_hl[t : t + NH, :, part, :].rearrange("t p n -> p t n")
                        tile = tile.rearrange("p (t n) -> p t n", t=NH)
                    sp.dma_start(dst, tile).then_inc(w2_out, 16)
            sp.wait_ge(w2_split, KT + 1)
            for part, tile in enumerate((wq1_high.bitcast(F32), wq1_raw)):
                sp.dma_start(qk_hl[HEADS, :, part, :], tile).then_inc(w2_out, 16)
            sp.wait_ge(w_split, KT + 1)
            sp.dma_start(v_hl.rearrange("p a (k n) -> p a k n", k=KT), w_v[:].bitcast(F32)).then_inc(wv_out, 16)

            with sp.Fori(0, B) as b:
                following = sp.snap((b + 1) % B)

                def wait_filled(what):
                    sp.wait_ge(filled[pair_of(what)], filling(b, what))

                def load_wqk(h, after):
                    s = slot_of(h)
                    wait_filled(after)
                    sp.dma_start(w_qk[s][:].bitcast(F32), qk_hl[h].rearrange("p a (k n) -> p a k n", k=KT)).then_inc(
                        wqk_loaded[s], 16
                    )

                def twins(h):
                    sp.wait_ge(drained["m1"], use(b, ("qk", h, 1), done=1))
                    sp.dma_start(q_hh[h % 2][D:P, :].bitcast(F32), q_hh[h % 2][0:D, :].bitcast(F32)).then_inc(qk_twin[h % 2], 16)
                    sp.dma_start(k_hl[h % 2][0:D, :].bitcast(F32), k_h1[h % 2][0:D, :].bitcast(F32)).then_inc(qk_twin[h % 2], 16)

                def max_row(h):
                    what = ("row", h)
                    sp.wait_ge(drained[pair_of(what)], use(b, what, done=1))
                    sp.dma_start(
                        q_lm[slot_of(h)][D : D + 1, :].rearrange("o (t p) -> o t p", p=P).bitcast(F32), row[:].bitcast(F32)
                    ).then_inc(row_back, 16)

                sp.wait_ge(norm_lo, (b + 1) * KT)
                sp.wait_ge(wqk_out, 2 * 16)
                sp.dma_start(w_qk[1][:].bitcast(F32), qk_hl[1].rearrange("p a (k n) -> p a k n", k=KT)).then_inc(
                    wqk_loaded[1], 16
                )
                twins(0)
                load_wqk(2, ("qk", 0, 1))
                max_row(0)
                twins(1)
                load_wqk(3, ("qk", 1, 1))

                def spread_denominators(h):
                    sp.wait_ge(drained["acc"], use(b, ("pv", h), done=1))
                    row = rows_of(h + 1).start
                    sp.dma_start(den_c[:], hf[row : row + 1, :]).then_inc(den_spread, 16)

                def return_inverses(h):
                    sp.wait_ge(rden_ready, b * (HEADS - 1) + h + 1)
                    sp.dma_start(rden_row[h % 2].rearrange("(p c) -> p c", p=P), rden_c[:]).then_inc(rden_out, 16)
                    if h % 2 == 0 and h:
                        wait_filled(("proj", h // 2 - 1, KT - 1, 1))
                        sp.dma_start(w_p[:].bitcast(F32), p_hl[h // 2]).then_inc(wp_loaded, 16)
                    sp.wait_ge(rden_out, 16 * (b * (HEADS - 1) + h + 1))
                    sp.dma_start(
                        hl[rows_of(h), :].bitcast(F32), rden_row[h % 2 : h % 2 + 1, :].to_broadcast([D, N])
                    ).then_inc(rden_back, 16)

                for h in range(1, HEADS):
                    max_row(h)
                    spread_denominators(h - 1)
                    if h + 1 < HEADS:
                        twins(h + 1)
                    if h + 3 < HEADS:
                        load_wqk(h + 3, ("qk", h + 1, 1))
                    if h == HEADS - 2:
                        load_wqk(0, ("qk", HEADS - 2, 1))
                        load_wqk(HEADS, ("qk", HEADS - 1, 1))
                    return_inverses(h - 1)
                    if h == 1:
                        sp.wait_ge(w2_out, (2 * KT + 2) * 16)
                        sp.wait_ge(wv_out, 16)
                        sp.dma_start(w_v[:].bitcast(F32), v1_hl.rearrange("p a (k n) -> p a k n", k=KT)).then_inc(
                            wv_loaded, 16
                        )
                        sp.dma_start(w_p[:].bitcast(F32), p_hl[0]).then_inc(wp_loaded, 16)
                    if h == PROJ_HEADS[0]:
                        what = ("proj", 0, KT - 1, 1)
                        sp.wait_ge(drained[pair_of(what)], use(b, what, done=1))
                        sp.dma_start(x_in[:], x[bass.ds(following, 1)].rearrange("b p k n -> (b p) k n")).then_inc(
                            x_loaded, 16
                        )
                max_row(HEADS)
                wait_filled(("v1", ST - 1))
                sp.dma_start(w_v[:].bitcast(F32), v_hl.rearrange("p a (k n) -> p a k n", k=KT)).then_inc(wv_loaded, 16)
                for n in range(NH):
                    sp.wait_ge(out_ready, 1 + b * NH + n + 1)
                    sp.dma_start(
                        out[bass.ds(b, 1)].rearrange("b p k n -> (b p) k n")[:, :, half(n)], x_mid[:, :, half(n)]
                    ).then_inc(out_done, 16)
            sp.wait_ge(x_loaded, (B + 1) * 16)
            sp.wait_ge(wqk_loaded[0], (B * HEADS // 2 + 2) * 16)
            sp.wait_ge(wv_loaded, (2 * B + 1) * 16)
            sp.wait_ge(out_done, 16 + B * NH * 16)

        @block.gpsimd
        def _(pool):
            pool.sem_inc(h_lo, 1)
            nc.gpsimd.memset(minus_half, -0.5)
            nc.gpsimd.memset(ones[:].bitcast(F32), 1.0)
            nc.gpsimd.memset(k_h1[0][:].bitcast(F32), 1.0)
            nc.gpsimd.memset(k_h1[1][:].bitcast(F32), 1.0).then_inc(ones_set, 1)
            pool.wait_ge(ones_set, 1)
            pool.wait_ge(drained["s1"], use(None, ("var",), done=1))
            nc.gpsimd.tensor_tensor(rstd_c, var_c, minus_half, ALU.pow).then_inc(rstd_ready, 1)
            for i, (raw, high) in enumerate((*zip(w2_raw, w2_high), (wq1_raw, wq1_high))):
                pool.wait_ge(w2_hi, i + 1)
                nc.gpsimd.tensor_tensor(raw, raw, high.bitcast(F32), ALU.subtract).then_inc(w2_split, 1)
            pool.wait_ge(wqk_out, 2 * 16)
            with pool.Fori(0, B) as b:
                pool.wait_ge(pv_done, 1 + b * TILES)
                nc.gpsimd.tensor_tensor(unused, minus_half, minus_half, ALU.add)
                for j in range(ST):
                    nc.gpsimd.memset(vh[:, j, :, 1, :].bitcast(F32), 1.0)
                    last = nc.gpsimd.memset(vl[:, j, :, 1, :].bitcast(F32), 0.0)
                last.then_inc(ones_set, 1)
                for h in range(HEADS - 1):
                    r = rows_of(h)
                    pool.wait_ge(rden_back, 16 * (b * (HEADS - 1) + h + 1))
                    nc.gpsimd.tensor_tensor(hf[r, :], hf[r, :], hl[r, :].bitcast(F32), ALU.mult).then_inc(h_scaled, 1)
                    pool.wait_ge(h_scaled, b * (HEADS - 1) + h + 1)
                    pool.wait_ge(h_hi, b * (HEADS - 1) + h + 1)
                    nc.gpsimd.tensor_tensor(hl[r, :], hf[r, :], hh[r, :].bitcast(F32), ALU.subtract).then_inc(h_lo, 1)
                    pool.wait_ge(h_lo, 1 + b * (HEADS - 1) + h + 1)
                r = rows_of(HEADS - 1)
                for i, c in enumerate(PIECES[:-1]):
                    pool.wait_ge(tail_hi, b * len(PIECES) + i + 1)
                    nc.gpsimd.tensor_tensor(hl[r, c], hf[r, c], hh[r, c].bitcast(F32), ALU.subtract).then_inc(tail_lo, 1)
                pool.wait_ge(tail_lo, (b + 1) * (len(PIECES) - 1))
                pool.wait_ge(drained["s1"], use(b, ("var",), done=1))
                nc.gpsimd.tensor_tensor(rstd_c, var_c, minus_half, ALU.pow).then_inc(rstd_ready, 1)

        @block.scalar
        def _(act):
            act.sem_inc(t1_drained, 1)
            act.wait_ge(wqk_in, 16)
            for i in range(KT):
                c = slice(i * N, (i + 1) * N)
                nc.scalar.activation(wqk_high[:, c], wqk_raw[:, c], ACT.Copy).then_inc(w_hi, 1)
            act.wait_ge(consts_in, 16 * 8)

            def norm_hi_part(image, k):
                act.wait_ge(y_ready, image * KT + k + 1)
                nc.scalar.activation(xh[:, k, :], y_of[k], ACT.Identity, bias=nb_c[:, k : k + 1]).then_inc(norm_hi, 1)

            for k in range(KT):
                norm_hi_part(0, k)
            act.wait_ge(wv_in, 16)
            nc.scalar.activation(w_v[:, 0], wv_f[:, 1], ACT.Copy).then_inc(w_hi, 1)
            act.wait_ge(w2_in, 3 * 16)
            for raw, high in (*zip(w2_raw, w2_high), (wq1_raw, wq1_high)):
                nc.scalar.activation(high, raw, ACT.Copy).then_inc(w2_hi, 1)

            with act.Fori(0, B) as b:

                def wait_filled(what, pair=None):
                    act.wait_ge(filled[pair or pair_of(what)], filling(b, what, pair))

                def exps(i, pair_drained, src, width, scale):
                    w = slice(0, width)
                    act.wait_ge(hi_done, 1 + b * TILES + max(i - 1, 0))
                    nc.scalar.activation(eh[i % 2][:, w], src, ACT.Exp, scale=scale).then_inc(e_hi, 1)
                    act.wait_ge(e_lo, 1 + b * TILES + i)
                    nc.scalar.activation(ef[:, w], src, ACT.Exp, scale=scale).then_inc(pair_drained, 1)

                def split_qk(h, n):
                    wait_filled(("qk", h, n))
                    c = half(n)
                    nc.scalar.activation(q_hh[h % 2][0:D, c], bank["misc"][0:D, c], ACT.Copy).then_inc(qk_hi, 1)
                    nc.scalar.activation(k_h1[h % 2][0:D, c], bank["misc"][D:P, c], ACT.Copy).then_inc(qk_hi, 1)

                def max_row(h):
                    wait_filled(("row", h))
                    act.wait_ge(row_back, 16 + 16 * (b * (HEADS + 1) + h))
                    pair = pair_of(("row", h))
                    nc.scalar.activation(row[:], bank[pair][0:ST, 0:P], ACT.Copy, scale=-1.0).then_inc(drained[pair], 1)

                def copy_head(h):
                    act.wait_ge(pv_done, 1 + b * TILES + (h + 1) * ST)
                    act.wait_ge(h_lo, 1 + b * (HEADS - 1) + h)
                    if h == 0:
                        act.wait_ge(out_ready, 1 + b * NH)
                    nc.scalar.activation(hf[:], bank["acc"][:], ACT.Copy).then_inc(drained["acc"], 1)

                def head_hi(h):
                    act.wait_ge(h_scaled, b * (HEADS - 1) + h + 1)
                    r = rows_of(h)
                    nc.scalar.activation(hh[r, :], hf[r, :], ACT.Copy).then_inc(h_hi, 1)

                for n in range(NH):
                    split_qk(0, n)
                act.wait_ge(wqk_out, 2 * 16)
                for j in range(ST):
                    wait_filled(("v", j))
                    nc.scalar.activation(
                        vh[:, j, :, 0:3:2, :],
                        bank[S[j % 2]][:, 0:C].rearrange("p (a c d) -> p a c d", c=2, d=D),
                        ACT.Copy,
                    ).then_inc(v_hi, 1)
                    if j == ROW_WITH_V:
                        max_row(0)
                for n in range(NH):
                    split_qk(1, n)
                act.wait_ge(w2_out, (2 * KT + 2) * 16)
                for h in range(HEADS):
                    for j in range(ST):
                        wait_filled(("s", h, j))
                        exps(h * ST + j, drained[S[j % 2]], bank[S[j % 2]][:], N, SCALE)
                        if j == 0 and 1 <= h < HEADS - 1:
                            split_qk(h + 1, 1)
                        if h and j == HEAD_HI_AT[(h - 1) % 2]:
                            head_hi(h - 1)
                    if h + 2 < HEADS:
                        max_row(h + 1)
                        split_qk(h + 2, 0)
                        copy_head(h)
                    elif h + 1 < HEADS:
                        max_row(h + 1)
                        copy_head(h)
                r = rows_of(HEADS - 1)
                for i, c in enumerate(PIECES):
                    if i < len(PIECES) - 1:
                        act.wait_ge(tail_scaled, b * (len(PIECES) - 1) + i + 1)
                    else:
                        act.wait_ge(drained["acc"], use(b, ("pv", HEADS - 1), done=1))
                    nc.scalar.activation(hh[r, c], hf[r, c], ACT.Copy).then_inc(tail_hi, 1)

                for n in range(NH):
                    for m in range(KT):
                        what = ("proj", LAST, m, n)
                        act.wait_ge(drained[pair_of(what)], use(b, what, done=1))
                        nc.scalar.activation(xh[:, m, half(n)], x_mid[:, m, half(n)], ACT.Copy).then_inc(mid_hi, 1)

                def split_g(n):
                    wait_filled(("g", n))
                    for dst, r in ((q_hh[1], slice(0, P)), (k_h1[1], slice(0, D)), (k_hl[1], slice(0, D))):
                        last = nc.scalar.activation(
                            dst[r, half(n)], bank["misc"][r, half(n)], ACT.Identity, bias=bq_c[r, :]
                        )
                    last.then_inc(g_hi, 1)

                split_g(0)
                for j in range(ST):
                    if j == 2:
                        split_g(1)
                    wait_filled(("v1", j))
                    nc.scalar.activation(
                        vh[:, j].rearrange("p a c d -> p (a c d)")[:, 0:C], bank[S[j % 2]][:, 0:C], ACT.Copy
                    ).then_inc(v_hi, 1)
                    if j == ROW_WITH_V:
                        max_row(HEADS)

                def copy_outputs(n):
                    if n == 0:
                        act.wait_ge(norm_lo, (b + 2) * KT)
                    else:
                        act.wait_ge(out_ready, 1 + b * NH + n)
                    wait_filled(("den", n))
                    nc.scalar.activation(hf[:, half(0)], bank["s1"][:, half(0)], ACT.Copy).then_inc(drained["s1"], 1)
                    wait_filled(("o", n), "acc")
                    nc.scalar.activation(hh_f[:], bank["acc"][:], ACT.Copy).then_inc(drained["acc"], 1)

                for i in range(NH * ST):
                    act.wait_ge(t1_filled, b * NH * ST + i + 1)
                    exps(HEADS * ST + i, t1_drained, bank["s0"][:, half(i % 2)], HALF, 1.0)
                    if i < ST:
                        for k in NORM_HI.get(i, ()):
                            norm_hi_part(b + 1, k)
                    if i == ST:
                        copy_outputs(0)
                copy_outputs(1)

        @block.vector
        def _(dve):
            dve.sem_inc(e_lo, 1)
            dve.sem_inc(out_ready, 1)
            for n in drained:
                dve.sem_inc(drained[n], 1)
            for i in range(KT):
                c = slice(i * N, (i + 1) * N)
                dve.wait_ge(w_hi, i + 1)
                nc.vector.tensor_tensor(
                    wqk_low[:, c], wqk_raw[:, c], wqk_high[:, c].bitcast(F32), ALU.subtract
                ).then_inc(w_split, 1)
            dve.wait_ge(consts_in, 16 * 8)
            first_links = [0]

            def first_link(ins):
                ins.then_inc(dve_step, 1)
                first_links[0] += 1
                dve.wait_ge(dve_step, first_links[0])

            first_link(nc.vector.tensor_scalar(gb_c, bv_c, gamma_c, None, ALU.mult))

            def statistics(i):
                k, n = divmod(i, NH)
                return nc.vector.bn_stats(stats[:, k, n, :], x_in[:, k, half(n)])

            def channel_moments(link, last_stats):
                link(last_stats)
                nc.vector.memset(dev_c, 0.0)
                for k in range(KT):
                    last = nc.vector.bn_aggr(mv[:, k, :], stats[:, k, :, :])
                last.then_inc(stat_ready, 1)

            def group_mean(b, image, link):
                dve.wait_ge(stat_ready, image * 2 + 1)
                dve.wait_ge(filled["s1"], filling(b, ("mean",)))
                nc.vector.tensor_copy(mean_c, bank["s1"][:, HALF : HALF + KT]).then_inc(drained["s1"], 1)
                dve.wait_ge(drained["s1"], use(b, ("mean",), done=1))
                link(nc.vector.tensor_tensor(dev_c, mv[:, :, 0], mean_c, ALU.subtract))
                link(nc.vector.tensor_tensor(dev_c, dev_c, dev_c, ALU.mult))
                nc.vector.tensor_tensor(dev_c, dev_c, mv[:, :, 1], ALU.add).then_inc(stat_ready, 1)

            def group_variance(b, image, link):
                dve.wait_ge(filled["s1"], filling(b, ("var",)))
                nc.vector.tensor_scalar(var_c, bank["s1"][:, HALF : HALF + KT], EPS, None, ALU.add).then_inc(
                    drained["s1"], 1
                )
                dve.wait_ge(rstd_ready, image + 1)
                link(nc.vector.tensor_tensor(fac_c, rstd_c, nw_c, ALU.mult))

            def norm_y(k):
                c = slice(k, k + 1)
                nc.vector.tensor_scalar(
                    y_of[k], x_in[:, k, :], mean_c[:, c], fac_c[:, c], ALU.subtract, ALU.mult
                ).then_inc(y_ready, 1)

            def norm_lo_part(image, k):
                dve.wait_ge(norm_hi, image * KT + k + 1)
                nc.vector.scalar_tensor_tensor(
                    out=xl[:, k, :], in0=y_of[k], scalar=nb_c[:, k : k + 1],
                    in1=xh[:, k, :].bitcast(F32), op0=ALU.add, op1=ALU.subtract,
                ).then_inc(norm_lo, 1)

            dve.wait_ge(x_loaded, 16)
            for i in range(KT * NH):
                last = statistics(i)
            channel_moments(first_link, last)
            group_mean(None, 0, first_link)
            group_variance(None, 0, first_link)
            for k in range(KT):
                norm_y(k)
            for k in range(KT):
                norm_lo_part(0, k)
            dve.wait_ge(w_hi, KT + 1)
            nc.vector.tensor_tensor(w_v[:, 1], wv_f[:, 1], w_v[:, 0].bitcast(F32), ALU.subtract).then_inc(
                w_split, 1
            )
            assert first_links[0] == START_LINKS, first_links

            with dve.Fori(0, B) as b:
                steps = [0]

                def link(ins):
                    ins.then_inc(dve_step, 1)
                    steps[0] += 1
                    dve.wait_ge(dve_step, b * DVE_LINKS + START_LINKS + steps[0])

                def wait_filled(what, pair=None):
                    dve.wait_ge(filled[pair or pair_of(what)], filling(b, what, pair))

                def drain(ins, what, pair=None):
                    ins.then_inc(drained[pair or pair_of(what)], 1)

                def exp_lo(i, pair_drained, done, width):
                    w = slice(0, width)
                    dve.wait_ge(pair_drained, done)
                    dve.wait_ge(pv_done, 1 + b * TILES + max(i - 1, 0))
                    nc.vector.tensor_tensor(
                        el[i % 2][:, w], ef[:, w], eh[i % 2][:, w].bitcast(F32), ALU.subtract
                    ).then_inc(e_lo, 1)

                def row_max(h, t):
                    if t % 2 and h in (0, HEADS):
                        what = ("max", h, t)
                        wait_filled(what)
                        ps = bank["acc"][:].rearrange("p (a n) -> p a n", a=NH)
                        drain(nc.vector.reduce_max(mx_half[:, t, :], ps, AX_X), what)
                    else:
                        for n in range(NH):
                            what = ("max", h, t, n)
                            wait_filled(what)
                            drain(nc.vector.reduce_max(mx_half[:, t, n : n + 1], bank["misc"][:, half(n)], AX_X), what)

                def full_max(h):
                    if h in (0, HEADS):
                        dve.wait_ge(drained["acc"], use(b, ("max", h, ST - 1), done=1))
                    dve.wait_ge(drained["m1"], use(b, ("max", h, ST - 1 if 0 < h < HEADS else ST - 2, 1), done=1))
                    nc.vector.tensor_tensor(mx[slot_of(h)][:], mx_half[:, :, 0], mx_half[:, :, 1], ALU.max).then_inc(
                        max_ready, 1
                    )
                    dve.wait_ge(max_ready, b * (HEADS + 1) + h + 1)

                def add_proj(p, m):
                    for n in range(NH):
                        what = ("proj", p, m, n)
                        wait_filled(what)
                        if p == 0 and m == 0 and n == 0:
                            dve.wait_ge(out_done, 16 + b * NH * 16)
                        ps, x_part = bank["misc"][:, half(n)], x_mid[:, m, half(n)]
                        if p == 0:
                            ins = nc.vector.scalar_tensor_tensor(
                                out=x_part, in0=ps, scalar=pb_c[:, m : m + 1], in1=x_in[:, m, half(n)],
                                op0=ALU.add, op1=ALU.add,
                            )
                        else:
                            ins = nc.vector.tensor_tensor(x_part, ps, x_part, ALU.add)
                        drain(ins, what)

                def lo_qk(h, n):
                    ps, s, c = bank["misc"], h % 2, half(n)
                    made = 2 * (b * HEADS * NH + h * NH + n)
                    dve.wait_ge(qk_hi, made + 1)
                    nc.vector.tensor_tensor(q_lm[s][0:D, c], ps[0:D, c], q_hh[s][0:D, c].bitcast(F32), ALU.subtract)
                    dve.wait_ge(qk_hi, made + 2)
                    drain(
                        nc.vector.tensor_tensor(
                            k_hl[s][D:P, c], ps[D:P, c], k_h1[s][0:D, c].bitcast(F32), ALU.subtract
                        ),
                        ("qk", h, n),
                    )

                def invert_denominators(h):
                    dve.wait_ge(den_spread, 16 * (b * (HEADS - 1) + h + 1))
                    nc.vector.reciprocal(rden_c[:], den_c[:]).then_inc(rden_ready, 1)

                for j in range(ST):
                    if j == 2:
                        for n in range(NH):
                            lo_qk(0, n)
                    dve.wait_ge(v_hi, b * 2 * ST + j + 1)
                    drain(
                        nc.vector.tensor_tensor(
                            vl[:, j, :, 0:3:2, :],
                            bank[S[j % 2]][:, 0:C].rearrange("p (a c d) -> p a c d", c=2, d=D),
                            vh[:, j, :, 0:3:2, :].bitcast(F32),
                            ALU.subtract,
                        ),
                        ("v", j),
                    )
                    for t in MAX_WITH_V.get(j, ()):
                        row_max(0, t)
                    if j == ROW_WITH_V - 1:
                        full_max(0)
                for n in range(NH):
                    lo_qk(1, n)
                for h in range(HEADS):
                    for j in range(ST):
                        if h + 1 < HEADS and j == ST - 1:
                            row_max(h + 1, j)
                            full_max(h + 1)
                        exp_lo(h * ST + j, drained[S[j % 2]], use(b, ("s", h, j), done=1), N)
                        if j == 0 and 1 <= h < HEADS - 1:
                            lo_qk(h + 1, 1)
                        if h and j == INVERT_AT:
                            invert_denominators(h - 1)
                        for what in extras(h, j) if j < ST - 1 else ():
                            (row_max if what[0] == "max" else add_proj)(*what[1:])
                        if h == HEADS - 1:
                            if j == 0:
                                dve.wait_ge(x_loaded, (b + 2) * 16)
                            for i in STATS_AT.get(j, ()):
                                last = statistics(i)
                            if j == max(STATS_AT):
                                channel_moments(link, last)
                    if h == HEADS - 2:
                        add_proj(LAST - 1, 0)
                    if h + 2 < HEADS:
                        lo_qk(h + 2, 0)

                dve.wait_ge(pv_done, 1 + b * TILES + HEADS * ST)
                r, den_rows = rows_of(HEADS - 1), rows_of(HEADS)
                for c in PIECES:
                    link(nc.vector.reciprocal(hf[r, c], bank["acc"][den_rows, c]))
                    nc.vector.tensor_tensor(hf[r, c], bank["acc"][r, c], hf[r, c], ALU.mult).then_inc(
                        drained["acc"] if c == PIECES[-1] else tail_scaled, 1
                    )
                dve.wait_ge(tail_hi, (b + 1) * len(PIECES))
                nc.vector.tensor_tensor(hl[r, c], hf[r, c], hh[r, c].bitcast(F32), ALU.subtract).then_inc(tail_end_lo, 1)

                for n in range(NH):
                    for m in range(KT):
                        what = ("proj", LAST, m, n)
                        wait_filled(what)
                        x_part = x_mid[:, m, half(n)]
                        ps = bank[("misc", "s0", "s1", "acc")[m]]
                        drain(nc.vector.tensor_tensor(x_part, ps[:, half(n)], x_part, ALU.add), what)
                    for m in range(KT):
                        dve.wait_ge(mid_hi, b * NH * KT + n * KT + m + 1)
                        nc.vector.tensor_tensor(
                            xl[:, m, half(n)], x_mid[:, m, half(n)], xh[:, m, half(n)].bitcast(F32), ALU.subtract
                        ).then_inc(mid_lo, 1)

                def lo_g(n):
                    dve.wait_ge(g_hi, b * NH + n + 1)
                    for dst, r in ((q_lm[1], slice(0, D)), (k_hl[1], slice(D, P))):
                        last = nc.vector.scalar_tensor_tensor(
                            out=dst[r, half(n)], in0=bank["misc"][r, half(n)], scalar=bq_c[r, :],
                            in1=q_hh[1][r, half(n)].bitcast(F32), op0=ALU.add, op1=ALU.subtract,
                        )
                    drain(last, ("g", n))

                lo_g(0)
                for j in range(ST):
                    if j == 2:
                        lo_g(1)
                    dve.wait_ge(v_hi, b * 2 * ST + ST + j + 1)
                    v_of = [t[:, j].rearrange("p a c d -> p (a c d)")[:, 0:C] for t in (vl, vh)]
                    drain(
                        nc.vector.tensor_tensor(v_of[0], bank[S[j % 2]][:, 0:C], v_of[1].bitcast(F32), ALU.subtract),
                        ("v1", j),
                    )
                    for t in MAX_WITH_V.get(j, ()):
                        row_max(HEADS, t)
                    if j == ROW_WITH_V - 1:
                        full_max(HEADS)
                def copy_outputs(n):
                    if n == 0:
                        dve.wait_ge(norm_lo, (b + 2) * KT)
                    dve.wait_ge(pv_done, 1 + b * TILES + (HEADS + n + 1) * ST)
                    for i in range(NH):
                        drain(nc.vector.tensor_copy(hl_f[:, half(i)], bank["misc"][:, half(i)]), ("o", n), MISC[i])
                    dve.wait_ge(drained["s1"], use(b, ("den", n), done=1))
                    link(nc.vector.reciprocal(hf[:, half(1)], hf[:, half(0)]))

                def output(n, m):
                    if m == 0:
                        link(nc.vector.tensor_scalar(hf[:, half(1)], hf[:, half(1)], gamma_c, None, ALU.mult))
                        dve.wait_ge(drained["acc"], use(b, ("o", n), "acc", done=1))
                    if m == KT // 2:
                        dve.wait_ge(drained["m1"], use(b, ("o", n), "m1", done=1))
                    return nc.vector.tensor_tensor(outs[m], outs[m], hf[:, half(1)], ALU.mult)

                def add_output(n, m):
                    last = nc.vector.scalar_tensor_tensor(
                        out=x_mid[:, m, half(n)], in0=outs[m], scalar=gb_c[:, m : m + 1],
                        in1=x_mid[:, m, half(n)], op0=ALU.add, op1=ALU.add,
                    )
                    if m == KT - 1:
                        last.then_inc(out_ready, 1)

                for n in range(NH):
                    for j in range(ST):
                        i = n * ST + j
                        exp_lo(HEADS * ST + i, t1_drained, 1 + b * NH * ST + i + 1, HALF)
                        if n == 0:
                            if j == MEAN_AT + 1:
                                group_mean(b, b + 1, link)
                            if j == VAR_AT + 1:
                                group_variance(b, b + 1, link)
                            for k in NORM_Y.get(j, ()):
                                if j == min(NORM_Y) and k == 0:
                                    dve.wait_ge(tail_lo, (b + 1) * (len(PIECES) - 1))
                                norm_y(k)
                            for k in NORM_LO.get(j, ()):
                                norm_lo_part(b + 1, k)
                        else:
                            if j == 0:
                                copy_outputs(0)
                            for m in OUTPUT_AT.get(j, ()):
                                link(output(0, m))
                                add_output(0, m)
                dve.wait_ge(out_ready, 1 + b * NH + 1)
                copy_outputs(1)
                for m in range(KT):
                    link(output(1, m))
                    add_output(1, m)
                dve.wait_ge(out_ready, 1 + (b + 1) * NH)
                assert steps[0] == DVE_LINKS, steps

        @block.tensor
        def _(pe):
            pe.sem_inc(hi_done, 1)
            pe.sem_inc(pv_done, 1)
            pe.wait_ge(consts_in, 16 * 8)
            pe.wait_ge(ones_set, 1)

            def group_average(b, what, image, values):
                pe.wait_ge(stat_ready, image * 2 + (1 if what == ("mean",) else 2))
                pe.wait_ge(drained["s1"], use(b, what))
                nc.tensor.matmul(bank["s1"][:, HALF : HALF + KT], grp[:], values, start=True, stop=True).then_inc(
                    filled["s1"], 1
                )

            group_average(None, ("mean",), 0, mv[:, :, 0])
            group_average(None, ("var",), 0, dev_c)
            pe.wait_ge(w_split, KT + 1)

            with pe.Fori(0, B) as b:

                def wait_free(what, pair=None):
                    pe.wait_ge(drained[pair or pair_of(what)], use(b, what, pair))

                def fill(ins, what, pair=None):
                    ins.then_inc(filled[pair or pair_of(what)], 1)

                def product(ps, hi_lo_pairs):
                    n = len(hi_lo_pairs)
                    for k, ((wh_, wl_), (mh, ml)) in enumerate(hi_lo_pairs):
                        nc.tensor.matmul(ps, wh_, mh, start=k == 0, stop=False)
                        nc.tensor.matmul(ps, wh_, ml, start=False, stop=False)
                        last = nc.tensor.matmul(ps, wl_, mh, start=False, stop=k == n - 1)
                    return last

                def project_v(j, what):
                    if what in (("v1", 0), ("v1", 1)):
                        pair = pair_of(what)
                        pe.wait_ge(drained[pair], use(b, ("proj", LAST, 1 + j, 1)))
                    else:
                        wait_free(what)
                    t = slice(j * P, (j + 1) * P)
                    fill(
                        product(
                            bank[pair_of(what)][:, 0:C],
                            [((xh[:, k, t], xl[:, k, t]), (w_v[:, 0, k, :], w_v[:, 1, k, :])) for k in range(KT)],
                        ),
                        what,
                    )

                def qk_half(h, n, within=lambda: None):
                    wait_free(("qk", h, n))
                    if n == 0:
                        loads = HEADS // 2 + h % 2
                        pe.wait_ge(wqk_loaded[h % 2], 16 * (b * loads + h // 2 + 1 + (h + 1) % 2))
                    w, ps = w_qk[h % 2], bank["misc"][:, half(n)]
                    for k in range(KT):
                        for i, (stat, moving) in enumerate(((0, xh), (0, xl), (1, xh))):
                            last = nc.tensor.matmul(
                                ps, w[:, stat, k, :], moving[:, k, half(n)],
                                start=k == 0 and i == 0, stop=k == KT - 1 and i == 2,
                            )
                        if k == 0:
                            within()
                    fill(last, ("qk", h, n))

                def max_tile(h, t):
                    s = slot_of(h)
                    on_acc = bool(t % 2) and h in (0, HEADS)
                    ps = bank["acc" if on_acc else "misc"]
                    if on_acc:
                        wait_free(("max", h, t))
                    for n in range(NH):
                        if not on_acc:
                            wait_free(("max", h, t, n))
                        last = nc.tensor.matmul(
                            ps[:, half(n)], q_hh[s][0:D, t * P : (t + 1) * P], k_h1[s][0:D, half(n)],
                            start=True, stop=True,
                        )
                        if not on_acc:
                            fill(last, ("max", h, t, n))
                    if on_acc:
                        fill(last, ("max", h, t))

                def max_row(h):
                    pe.wait_ge(max_ready, b * (HEADS + 1) + h + 1)
                    wait_free(("row", h))
                    fill(nc.tensor.transpose(bank[pair_of(("row", h))][0:ST, 0:P], mx[slot_of(h)][:], eye[:]), ("row", h))

                def wait_row(h):
                    pe.wait_ge(row_back, 16 + 16 * (b * (HEADS + 1) + h + 1))

                def scores(s, ps, j, n):
                    keys = slice(j * P, (j + 1) * P)
                    nc.tensor.matmul(ps, k_hl[s][:, keys], q_hh[s][:, half(n)], start=True, stop=False)
                    return nc.tensor.matmul(
                        ps, k_h1[s][0 : D + 1, keys], q_lm[s][0 : D + 1, half(n)], start=False, stop=True
                    )

                def head_scores(h, j):
                    what = ("s", h, j)
                    wait_free(what)
                    if j == 0:
                        wait_row(h)
                        pe.wait_ge(qk_twin[h % 2], 32 * (b * (HEADS // 2) + h // 2 + 1))
                        pe.wait_ge(drained["m1"], use(b, ("qk", h, 1), done=1))
                    for n in range(NH):
                        last = scores(h % 2, bank[S[j % 2]][:, half(n)], j, n)
                    fill(last, what)

                def head_pv_hi(h, j):
                    i = h * ST + j
                    if j == 0:
                        wait_free(("pv", h))
                    pe.wait_ge(e_hi, b * TILES + i + 1)
                    for n in range(NH):
                        ps, moving = bank["acc"][:, half(n)], eh[i % 2][:, half(n)]
                        nc.tensor.matmul(ps, head_v(vh, h, j), moving, start=j == 0, stop=False)
                        last = nc.tensor.matmul(ps, head_v(vl, h, j), moving, start=False, stop=False)
                    last.then_inc(hi_done, 1)

                def head_pv_lo(h, j):
                    i = h * ST + j
                    pe.wait_ge(e_lo, 1 + b * TILES + i + 1)
                    for n in range(NH):
                        last = nc.tensor.matmul(
                            bank["acc"][:, half(n)], head_v(vh, h, j), el[i % 2][:, half(n)],
                            start=False, stop=j == ST - 1,
                        )
                    last.then_inc(pv_done, 1)

                def project_columns(p, m, c):
                    w = slice(m * P, (m + 1) * P)
                    ps = bank["misc" if p < LAST or m == 0 else pair_of(("proj", p, m, 0))]
                    return product(ps[:, c], [((w_p[:, 0, w], w_p[:, 1, w]), (hh[:, c], hl[:, c]))])

                def project_out(p, m):
                    if m == 0:
                        pe.wait_ge(wp_loaded, 16 * (b * KT + p + 1))
                        pe.wait_ge(h_lo, 1 + b * (HEADS - 1) + 2 * p + 2)
                    for n in range(NH):
                        wait_free(("proj", p, m, n))
                        fill(project_columns(p, m, half(n)), ("proj", p, m, n))

                pe.wait_ge(norm_lo, (b + 1) * KT)
                for n in range(NH):
                    qk_half(0, n)
                pe.wait_ge(wv_loaded, 16 * (2 * b + 1))
                pe.wait_ge(t1_drained, 1 + b * NH * ST)
                for j in range(ST):
                    project_v(j, ("v", j))
                    for t in MAX_WITH_V.get(j, ()):
                        max_tile(0, t)
                    if j == ROW_WITH_V:
                        max_row(0)
                for n in range(NH):
                    qk_half(1, n)
                pe.wait_ge(ones_set, b + 2)
                head_scores(0, 0)
                for h in range(HEADS):
                    for j in range(ST):
                        if j + 1 < ST:
                            head_scores(h, j + 1)
                        for what in extras(h, j):
                            if what[0] == "proj":
                                project_out(*what[1:])
                        head_pv_hi(h, j)
                        if h + 1 < HEADS:
                            max_tile(h + 1, j)
                        if j:
                            head_pv_lo(h, j - 1)
                    if h + 2 < HEADS:
                        qk_half(h + 2, 0, within=lambda: max_row(h + 1))
                    elif h + 1 < HEADS:
                        max_row(h + 1)
                    if h == HEADS - 2:
                        project_out(LAST - 1, 0)
                    head_pv_lo(h, ST - 1)
                    if h + 1 < HEADS:
                        head_scores(h + 1, 0)
                    if h + 2 < HEADS:
                        qk_half(h + 2, 1)

                pe.wait_ge(wp_loaded, 16 * (b + 1) * KT)
                pe.wait_ge(h_lo, 1 + (b + 1) * (HEADS - 1))
                for i, c in enumerate(PIECES[:-1]):
                    pe.wait_ge(tail_lo, b * (len(PIECES) - 1) + i + 1)
                    for m in range(KT - 1):
                        if i == 0:
                            wait_free(("proj", LAST, m, 0))
                        last = project_columns(LAST, m, c)
                        if c.stop == HALF:
                            fill(last, ("proj", LAST, m, 0))
                wait_free(("proj", LAST, KT - 1, 0))
                fill(project_columns(LAST, KT - 1, half(0)), ("proj", LAST, KT - 1, 0))
                pe.wait_ge(tail_end_lo, b + 1)
                for m in range(KT):
                    if m == 0:
                        wait_free(("proj", LAST, m, 1))
                    fill(project_columns(LAST, m, half(1)), ("proj", LAST, m, 1))

                def project_g(n):
                    if n == 0:
                        pe.wait_ge(wqk_loaded[1], 16 * (b + 1) * (HEADS // 2 + 1))
                    wait_free(("g", n))
                    w = w_qk[1]
                    for k in range(KT):
                        pe.wait_ge(mid_lo, b * NH * KT + n * KT + k + 1)
                        for i, (stat, moving) in enumerate(((0, xh), (0, xl), (1, xh))):
                            last = nc.tensor.matmul(
                                bank["misc"][:, half(n)], w[:, stat, k, :], moving[:, k, half(n)],
                                start=k == 0 and i == 0, stop=k == KT - 1 and i == 2,
                            )
                    fill(last, ("g", n))

                project_g(0)
                pe.wait_ge(wv_loaded, 16 * (2 * b + 2))
                for j in range(ST):
                    if j == 2:
                        project_g(1)
                    project_v(j, ("v1", j))
                    for t in MAX_WITH_V.get(j, ()):
                        max_tile(HEADS, t)
                    if j == ROW_WITH_V:
                        max_row(HEADS)

                def scores1(i):
                    n, j = divmod(i, ST)
                    if i == 0:
                        wait_row(HEADS)
                        pe.wait_ge(drained["s0"], use(b, ("v1", ST - 2), done=1))
                    pe.wait_ge(t1_drained, 1 + b * NH * ST + max(i - 1, 0))
                    scores(1, bank["s0"][:, half(i % 2)], j, n).then_inc(t1_filled, 1)

                den = bank["s1"][:, half(0)]

                def out_of(m):
                    return bank[("acc", "misc")[m // 2]][:, half(m % 2)]

                def v1_of(tile, j, m):
                    return tile[:, j].rearrange("p a c d -> p (a c d)")[:, m * P : (m + 1) * P]

                def pv_hi1(n, j):
                    i = HEADS * ST + n * ST + j
                    if j == 0:
                        wait_free(("o", n), "acc")
                        wait_free(("o", n), "m0")
                        wait_free(("o", n), "m1")
                        wait_free(("mean",) if n == 0 else ("den", n))
                    pe.wait_ge(e_hi, b * TILES + i + 1)
                    moving = eh[i % 2][:, 0:HALF]
                    nc.tensor.matmul(den, ones[:], moving, start=j == 0, stop=False)
                    for m in range(KT):
                        nc.tensor.matmul(out_of(m), v1_of(vh, j, m), moving, start=j == 0, stop=False)
                        last = nc.tensor.matmul(out_of(m), v1_of(vl, j, m), moving, start=False, stop=False)
                    last.then_inc(hi_done, 1)

                def pv_lo1(n, j):
                    i = HEADS * ST + n * ST + j
                    end = j == ST - 1
                    pe.wait_ge(e_lo, 1 + b * TILES + i + 1)
                    moving = el[i % 2][:, 0:HALF]
                    last = nc.tensor.matmul(den, ones[:], moving, start=False, stop=end)
                    if end:
                        fill(last, ("den", n))
                    for m in range(KT):
                        last = nc.tensor.matmul(out_of(m), v1_of(vh, j, m), moving, start=False, stop=end)
                        if end and m == 1:
                            fill(last, ("o", n), "acc")
                    last.then_inc(pv_done, 1)

                scores1(0)
                for n in range(NH):
                    for j in range(ST):
                        if n * ST + j + 1 < NH * ST:
                            scores1(n * ST + j + 1)
                        pv_hi1(n, j)
                        if j:
                            pv_lo1(n, j - 1)
                        if n == 0 and j == MEAN_AT:
                            group_average(b, ("mean",), b + 1, mv[:, :, 0])
                        if n == 0 and j == VAR_AT:
                            group_average(b, ("var",), b + 1, dev_c)
                    pv_lo1(n, ST - 1)


def kernel(x, L0_conv_norm_w, L0_conv_norm_b, L0_conv_qkv_w, L0_conv_proj_w, L0_conv_proj_b, L1_conv_Wq, L1_conv_bq, L1_conv_Wv, L1_conv_bv, L1_conv_gamma):
    import concourse.bacc as bacc
    from concourse.bass_utils import run_bass_kernel_spmd

    def array(a):
        return np.ascontiguousarray(np.asarray(a))

    def by_channel(v):
        return array(v).reshape(KT, P).T

    def stationary(w):
        return array(w).reshape(-1, KT, P).transpose(2, 1, 0)

    qkv = array(L0_conv_qkv_w).reshape(HEADS, 3 * D, C)
    arrays = {
        "x": array(x).reshape(B, C, N),
        "wqk": qkv[:, 0 : 2 * D].reshape(HEADS, 2 * D, KT, P).transpose(3, 0, 2, 1).reshape(P, -1),
        "wv": stationary(qkv[:, 2 * D :].reshape(C, C)).reshape(P, -1),
        "wv1": stationary(L1_conv_Wv).reshape(P, -1),
        "wp": stationary(L0_conv_proj_w).reshape(P, -1),
        "wq1": stationary(np.concatenate([array(L1_conv_Wq)] * 2)).reshape(P, -1),
        "pb": by_channel(L0_conv_proj_b),
        "norm_w": by_channel(L0_conv_norm_w),
        "norm_b": by_channel(L0_conv_norm_b),
        "bv1": by_channel(L1_conv_bv),
        "bq1": np.concatenate([array(L1_conv_bq)] * 2).reshape(P, 1),
        "gamma": np.repeat(array(L1_conv_gamma), P).reshape(P, 1),
        "group": np.kron(np.eye(P * GROUPS // C), np.full((C // GROUPS,) * 2, GROUPS / C)).astype(np.float32),
        "ident": np.eye(P, dtype=np.float32),
    }
    nc = bacc.Bacc("TRN2", target_bir_lowering=False, num_devices=1)
    arrays = {f"in_{n}": array(a) for n, a in arrays.items()}
    aps = [nc.dram_tensor(n, a.shape, F32, kind="ExternalInput").ap() for n, a in arrays.items()]
    out = nc.dram_tensor("out", (B, C, N), F32, kind="ExternalOutput").ap()
    aps[0], out = (a.rearrange("b (k p) n -> b p k n", p=P) for a in (aps[0], out))
    attention_kernel(nc, *aps, out)
    result = run_bass_kernel_spmd(nc, [arrays], core_ids=[0])
    return result.results[0]["out"].reshape(np.shape(x))
```
